# Optimizing a Trainium2 kernel written in Bass

```python
import numpy as np
import jax
import jax.numpy as jnp

def _softmax(x, axis=-1):
    return jax.nn.softmax(x, axis=axis)

def _gelu(x):
    return jax.nn.gelu(x, approximate=True)

def _silu(x):
    return jax.nn.silu(x)

def _sigmoid(x):
    return jax.nn.sigmoid(x)

def _layernorm(x, axis=-1, eps=1e-05):
    m = jnp.mean(x, axis=axis, keepdims=True)
    v = jnp.var(x, axis=axis, keepdims=True)
    return (x - m) / jnp.sqrt(v + eps)

def _scatter_add(tgt, idx, src, axis=0):
    return tgt.at[idx].add(src)

def _segment_sum(src, seg, n):
    return jax.ops.segment_sum(src, seg, n)
kernel_name = 'mk_gnn_preln_d4_gnn_r32_33dd9b'

def setup_inputs(seed: int=0):
    np.random.seed(seed)
    _w = jnp.asarray

    def _rec_inputs():
        import jax
        import jax.numpy as jnp
        _gk = jax.random.key(seed)
        x = -0.000202 + 1 * jax.random.normal(jax.random.fold_in(_gk, 1), (3125, 64), jnp.float32)
        _s = jax.random.randint(jax.random.fold_in(_gk, 2), (50000,), 0, 3125, jnp.int32)
        _d = jax.random.randint(jax.random.fold_in(_gk, 3), (50000,), 0, 3125, jnp.int32)
        _loop = jnp.arange(3125, dtype=jnp.int32)
        src = jnp.concatenate([_s, _d, _loop])
        dst = jnp.concatenate([_d, _s, _loop])
        _o = jnp.argsort(dst, stable=True)
        src = src[_o]
        dst = dst[_o]
        edge_attr_16 = 0.000196303 + 1.00016 * jax.random.normal(jax.random.fold_in(_gk, 11), (103125, 16), jnp.float32)
        edge_attr_32 = 0.000189758 + 1.00013 * jax.random.normal(jax.random.fold_in(_gk, 12), (103125, 32), jnp.float32)
        return (x, src, dst, edge_attr_16, edge_attr_32)
    x, src, dst, edge_attr_16, edge_attr_32 = _rec_inputs()

    def _L0_gnn_setup():
        import jax, jax.numpy as jnp
        import numpy as np
        N_NODES = 3125
        N_EDGES = 50000
        IN_CH = 64
        OUT_CH = 64
        EDGE_DIM = 16
        key = jax.random.key(seed)
        ks = jax.random.split(key, 8)
        x = jax.random.normal(ks[0], (N_NODES, IN_CH), dtype=jnp.float32)
        edge_index = jax.random.randint(ks[1], (2, N_EDGES), 0, N_NODES, dtype=jnp.int64)
        edge_attr = jax.random.normal(ks[2], (N_EDGES, EDGE_DIM), dtype=jnp.float32)
        W_l = jax.random.normal(ks[3], (IN_CH, OUT_CH), dtype=jnp.float32) / np.sqrt(IN_CH)
        b_l = jnp.zeros((OUT_CH,), dtype=jnp.float32)
        W_r = jax.random.normal(ks[4], (IN_CH, OUT_CH), dtype=jnp.float32) / np.sqrt(IN_CH)
        W_e = jax.random.normal(ks[5], (EDGE_DIM, OUT_CH), dtype=jnp.float32) / np.sqrt(EDGE_DIM)
        b_e = jax.random.normal(ks[6], (OUT_CH,), dtype=jnp.float32) * 0.01
        return {'x': x, 'edge_index': edge_index, 'edge_attr': edge_attr, 'W_l': W_l, 'b_l': b_l, 'W_r': W_r, 'W_e': W_e, 'b_e': b_e}
    _L0_gnn_all = _L0_gnn_setup()
    _L0_gnn_in = {k: v for k, v in _L0_gnn_all.items() if k in ('W_l', 'b_l', 'W_r', 'W_e', 'b_e')}
    del _L0_gnn_all

    def _L1_gnn_setup():
        import jax, jax.numpy as jnp
        import numpy as np
        N_NODES = 3125
        N_EDGES = 50000
        IN_CH = 64
        OUT_CH = 64
        key = jax.random.key(seed)
        k_x, k_e, k_w, k_b = jax.random.split(key, 4)
        x = jax.random.normal(k_x, (N_NODES, IN_CH), dtype=jnp.float32)
        edge_index = jax.random.randint(k_e, (2, N_EDGES), 0, N_NODES, dtype=jnp.int64)
        limit = float(np.sqrt(6.0 / (IN_CH + OUT_CH)))
        W = jax.random.uniform(k_w, (IN_CH, OUT_CH), dtype=jnp.float32, minval=-limit, maxval=limit)
        b = jnp.zeros((OUT_CH,), dtype=jnp.float32)
        return {'x': x, 'edge_index': edge_index, 'W': W, 'b': b}
    _L1_gnn_all = _L1_gnn_setup()
    _L1_gnn_in = {k: v for k, v in _L1_gnn_all.items() if k in ('W', 'b')}
    del _L1_gnn_all

    def _L2_gnn_setup():
        import jax, jax.numpy as jnp
        import numpy as np
        N_NODES = 50000
        N_EDGES = 25000
        N_FEAT = 64
        N_LAYERS = 3
        key = jax.random.key(seed)
        k1, k2, k3 = jax.random.split(key, 3)
        x = jax.random.normal(k1, (N_NODES, N_FEAT), dtype=jnp.float32)
        edge_index = jax.random.randint(k2, (2, N_EDGES), 0, N_NODES, dtype=jnp.int64)
        bound = 1.0 / np.sqrt(N_FEAT)
        weights = jax.random.uniform(k3, (N_LAYERS, N_FEAT, N_FEAT), dtype=jnp.float32, minval=-bound, maxval=bound)
        return {'x': x, 'edge_index': edge_index, 'weights': weights}
    _L2_gnn_all = _L2_gnn_setup()
    _L2_gnn_in = {k: v for k, v in _L2_gnn_all.items() if k in ('weights',)}
    del _L2_gnn_all

    def _L3_gnn_setup():
        import jax, jax.numpy as jnp
        import numpy as np
        N_NODES = 3125
        N_EDGES = 50000
        NODE_F = 64
        EDGE_F = 32
        BN_EPS = 1e-05
        key = jax.random.key(seed)
        ks = jax.random.split(key, 8)
        in_dim = 2 * NODE_F + EDGE_F
        scale = 1.0 / np.sqrt(in_dim)
        return {'node_attrs': jax.random.normal(ks[0], (N_NODES, NODE_F), jnp.float32), 'edge_index': jax.random.randint(ks[1], (2, N_EDGES), 0, N_NODES, jnp.int64), 'edge_attrs': jax.random.normal(ks[2], (N_EDGES, EDGE_F), jnp.float32), 'W_f': jax.random.normal(ks[3], (in_dim, NODE_F), jnp.float32) * scale, 'b_f': jnp.zeros((NODE_F,), jnp.float32), 'W_s': jax.random.normal(ks[4], (in_dim, NODE_F), jnp.float32) * scale, 'b_s': jnp.zeros((NODE_F,), jnp.float32), 'gamma': jnp.ones((NODE_F,), jnp.float32), 'beta': jnp.zeros((NODE_F,), jnp.float32)}
    _L3_gnn_all = _L3_gnn_setup()
    _L3_gnn_in = {k: v for k, v in _L3_gnn_all.items() if k in ('W_f', 'b_f', 'W_s', 'b_s', 'gamma', 'beta')}
    del _L3_gnn_all
    return {'x': x, 'src': src, 'dst': dst, 'edge_attr_16': edge_attr_16, 'edge_attr_32': edge_attr_32, 'L0_gnn_W_l': _L0_gnn_in['W_l'], 'L0_gnn_b_l': _L0_gnn_in['b_l'], 'L0_gnn_W_r': _L0_gnn_in['W_r'], 'L0_gnn_W_e': _L0_gnn_in['W_e'], 'L0_gnn_b_e': _L0_gnn_in['b_e'], 'L1_gnn_W': _L1_gnn_in['W'], 'L1_gnn_b': _L1_gnn_in['b'], 'L2_gnn_weights': _L2_gnn_in['weights'], 'L3_gnn_W_f': _L3_gnn_in['W_f'], 'L3_gnn_b_f': _L3_gnn_in['b_f'], 'L3_gnn_W_s': _L3_gnn_in['W_s'], 'L3_gnn_b_s': _L3_gnn_in['b_s'], 'L3_gnn_gamma': _L3_gnn_in['gamma'], 'L3_gnn_beta': _L3_gnn_in['beta']}

def reference(x, src, dst, edge_attr_16, edge_attr_32, L0_gnn_W_l, L0_gnn_b_l, L0_gnn_W_r, L0_gnn_W_e, L0_gnn_b_e, L1_gnn_W, L1_gnn_b, L2_gnn_weights, L3_gnn_W_f, L3_gnn_b_f, L3_gnn_W_s, L3_gnn_b_s, L3_gnn_gamma, L3_gnn_beta):
    import jax
    import jax.numpy as jnp

    def _L0_gnn_ref(x, edge_index, edge_attr, W_l, b_l, W_r, W_e, b_e):
        import jax, jax.numpy as jnp
        import numpy as np
        N_NODES = 3125
        N_EDGES = 50000
        IN_CH = 64
        OUT_CH = 64
        EDGE_DIM = 16
        N = x.shape[0]
        row, col = (edge_index[0], edge_index[1])
        x_j = x[row]
        agg = jax.ops.segment_sum(x_j, col, num_segments=N)
        cnt = jax.ops.segment_sum(jnp.ones((row.shape[0],), x.dtype), col, num_segments=N)
        mean = agg / jnp.maximum(cnt, 1.0)[:, None]
        out = mean @ W_l + b_l + x @ W_r
        e = edge_attr @ W_e + b_e
        out = out + jnp.zeros_like(out).at[col].set(e)
        return out

    def _L1_gnn_ref(x, edge_index, W, b):
        import jax, jax.numpy as jnp
        import numpy as np
        N_NODES = 3125
        N_EDGES = 50000
        IN_CH = 64
        OUT_CH = 64
        N = x.shape[0]
        loop = jnp.arange(N, dtype=edge_index.dtype)
        src = jnp.concatenate([edge_index[0], loop])
        dst = jnp.concatenate([edge_index[1], loop])
        ew = jnp.ones(src.shape[0], dtype=x.dtype)
        deg = jax.ops.segment_sum(ew, dst, num_segments=N)
        dinv = jnp.where(deg > 0, jax.lax.rsqrt(deg), jnp.zeros_like(deg))
        norm = dinv[src] * dinv[dst]
        h = x @ W
        msg = h[src] * norm[:, None]
        out = jax.ops.segment_sum(msg, dst, num_segments=N)
        return out + b

    def _L2_gnn_ref(x, edge_index, weights):
        import jax, jax.numpy as jnp
        import numpy as np
        N_NODES = 50000
        N_EDGES = 25000
        N_FEAT = 64
        N_LAYERS = 3
        n = x.shape[0]
        self_idx = jnp.arange(n, dtype=edge_index.dtype)
        src = jnp.concatenate([edge_index[0], self_idx])
        dst = jnp.concatenate([edge_index[1], self_idx])
        deg = jax.ops.segment_sum(jnp.ones(src.shape[0], dtype=x.dtype), dst, num_segments=n)
        inv_deg = (1.0 / jnp.maximum(deg, 1.0))[:, None]
        for l in range(weights.shape[0]):
            agg = jax.ops.segment_sum(x[src], dst, num_segments=n) * inv_deg
            x = agg @ weights[l].T
        return x

    def _L3_gnn_ref(node_attrs, edge_index, edge_attrs, W_f, b_f, W_s, b_s, gamma, beta):
        import jax, jax.numpy as jnp
        import numpy as np
        N_NODES = 3125
        N_EDGES = 50000
        NODE_F = 64
        EDGE_F = 32
        BN_EPS = 1e-05
        source, target = (edge_index[0], edge_index[1])
        x_i = node_attrs[source]
        x_j = node_attrs[target]
        z = jnp.concatenate([x_i, x_j, edge_attrs], axis=-1)
        h = jax.nn.sigmoid(z @ W_f + b_f) * jax.nn.softplus(z @ W_s + b_s)
        message = jax.ops.segment_sum(h, source, num_segments=node_attrs.shape[0])
        mean = jnp.mean(message, axis=0)
        var = jnp.mean((message - mean) ** 2, axis=0)
        normed = (message - mean) * jax.lax.rsqrt(var + BN_EPS) * gamma + beta
        return node_attrs + normed
    edge_index = jnp.stack([src, dst])
    h = jnp.maximum(_layernorm(x, axis=-1), 0.0)
    x = x + _L0_gnn_ref(h, edge_index, edge_attr_16, L0_gnn_W_l, L0_gnn_b_l, L0_gnn_W_r, L0_gnn_W_e, L0_gnn_b_e)
    h = jnp.maximum(_layernorm(x, axis=-1), 0.0)
    x = x + _L1_gnn_ref(h, edge_index, L1_gnn_W, L1_gnn_b)
    h = jnp.maximum(_layernorm(x, axis=-1), 0.0)
    x = x + _L2_gnn_ref(h, edge_index, L2_gnn_weights)
    h = jnp.maximum(_layernorm(x, axis=-1), 0.0)
    x = x + _L3_gnn_ref(h, edge_index, edge_attr_32, L3_gnn_W_f, L3_gnn_b_f, L3_gnn_W_s, L3_gnn_b_s, L3_gnn_gamma, L3_gnn_beta)
    return x

_drawn_inputs = setup_inputs


def setup_inputs(seed=0):
    import zlib

    import numpy as np

    out = dict(_drawn_inputs(seed))
    spreads = {'L0_gnn_b_l': (0.0, 0.1),
     'L1_gnn_b': (0.0, 0.1),
     'L3_gnn_b_f': (0.0, 0.8),
     'L3_gnn_b_s': (0.0, 0.8),
     'L3_gnn_gamma': (1.0, 0.2),
     'L3_gnn_beta': (0.0, 0.275)}
    factors = {'L0_gnn_b_e': 8.0}
    for name, (base, spread) in spreads.items():
        noise = np.random.default_rng([zlib.crc32(name.encode()), seed]).standard_normal(out[name].shape)
        drawn = base * np.exp(spread * noise) if base else spread * noise
        out[name] = jnp.asarray(drawn.astype(out[name].dtype))
    for name, factor in factors.items():
        out[name] = (out[name] * factor).astype(out[name].dtype)
    return out
```

```python
import concourse.bass as bass
from concourse import mybir
from concourse.bass import ds
from contextlib import ExitStack

N_NODES = 3125
FEAT = 64
N_EDGES = 103125
P = 128
TILES = -(-N_NODES // P)
NPAD = TILES * P
LAST = N_NODES - (TILES - 1) * P
CHUNKS = -(-N_EDGES // (8 * P)) * 8
PAIRS = CHUNKS // 2
PAIRS_PER_ROW = 4
PAIR_ROWS = PAIRS // PAIRS_PER_ROW
QUADS = CHUNKS // 4
EDGE_F = 32
EDGE_D = 16
LAYERS = 5
GROUPS = -(-TILES // 4)
ECAT = EDGE_D + 2
PAD = 4095
ARENA = 18600


def gnn_program(nc, x, src_cols, dst_cols, dst_rows, e16, e32t, sage_wl, sage_bl, sage_wr, sage_we,
                sage_be, gcn_w, gcn_b, mean_wt, wf, bf_, ws, bs_, gamma, beta, out):
    f32, bf16, i32, i16 = mybir.dt.float32, mybir.dt.bfloat16, mybir.dt.int32, mybir.dt.int16
    ALU, ACT, AX = mybir.AluOpType, mybir.ActivationFunctionType, mybir.AxisListType

    table_p = nc.dram_tensor("table_p", [NPAD, 2 * FEAT], f32, kind="Internal").ap()
    table_q = nc.dram_tensor("table_q", [NPAD, 2 * FEAT], f32, kind="Internal").ap()

    with ExitStack() as ctx:
        def sb(name, shape, dt):
            return ctx.enter_context(nc.sbuf_tensor(name, shape, dt))

        def sem(name):
            return ctx.enter_context(nc.semaphore(name))

        adj = sb("adj", [P, TILES * NPAD], bf16)
        arena = sb("arena", [P, ARENA], bf16)
        A3 = adj[:, :].rearrange("p (k d) -> p k d", k=TILES)

        def views(base, wanted, limit):
            found, at = {}, 0
            for name, words, dt in wanted:
                v = base[:, at:at + 2 * words]
                found[name] = v if dt == bf16 else v.bitcast(dt)
                at += 2 * words
            assert at <= limit, at
            return found

        B = views(arena, [("node_iota", NPAD // 2, i16), ("srcf", CHUNKS, f32), ("dstf", CHUNKS, f32),
                          ("oh_src", NPAD, bf16), ("oh_dst", P, bf16), ("later", CHUNKS, f32),
                          ("flag_ids", CHUNKS * 3 // 2, bf16), ("zeros", 256, bf16)], ARENA)
        oh_src = B["oh_src"].rearrange("p (s n) -> p s n", s=2)
        oh_dst = B["oh_dst"].rearrange("p (s n) -> p s n", s=2)
        flag_ids = B["flag_ids"].rearrange("p (c k) -> p c k", k=3)
        S = views(adj, [("src_i", CHUNKS, i32), ("dst_i", CHUNKS, i32), ("drow", 2 * 512, i32),
                        ("ids_i", CHUNKS * 3, i32), ("ids", CHUNKS * 3 // 2, bf16), ("junk", P, bf16),
                        ("pair_dst", PAIRS_PER_ROW * 256, i32)], TILES * NPAD)
        L = views(arena, [("x", TILES * FEAT, f32), ("h", TILES * FEAT, f32), ("t", TILES * FEAT, f32),
                          ("y12", TILES * FEAT, bf16), ("y3", TILES * 33, bf16),
                          ("t12", 1024, f32), ("t3", 1024, f32)], ARENA)
        xs, hs, ts = (L[k].rearrange("p (t f) -> p t f", f=FEAT) for k in ("x", "h", "t"))
        y12 = L["y12"].rearrange("p (t f) -> p t f", f=2 * FEAT)
        y3 = L["y3"].rearrange("p (t f) -> p t f", f=66)
        t12 = L["t12"].rearrange("p (s n) -> p s n", s=2)
        t3 = L["t3"].rearrange("p (s n) -> p s n", s=2)
        SLOTS = 8
        M = views(adj, [("node_iota", NPAD // 2, i16), ("srcf", CHUNKS, f32), ("src_i", CHUNKS, i32),
                        ("dst_i", CHUNKS, i32), ("oh", SLOTS * NPAD // 2, bf16), ("e_t", 2 * 512, f32),
                        ("gp", 2 * 512, f32), ("gq", 2 * 512, f32), ("z", 2 * 512, f32),
                        ("en", 2 * 256, f32), ("ab", 2 * 256, f32), ("ln", 2 * 256, f32),
                        ("hm", 2 * 256, f32), ("m1", 256, bf16), ("m2", 256, bf16), ("m3", 256, bf16),
                        ("msg", TILES * FEAT, f32), ("pq", 2 * 256, f32), ("zeros", 256, bf16),
                        ("now", 16, i32)], TILES * NPAD)

        ident = sb("ident", [P, P], f32)
        ident16 = sb("ident16", [P, P], bf16)
        after = sb("after", [P, P], f32)
        ones = sb("ones", [P, P], f32)
        last_id = sb("last_id", [P, TILES], f32)
        cnt = sb("cnt", [P, TILES], f32)
        scale = sb("scale", [P, 3, TILES], f32)
        stat = sb("stat", [P, 3, TILES], f32)
        gat_i = sb("gat_i", [P, TILES], i32)
        w12 = sb("w12", [P, LAYERS, 65], f32)
        w3 = sb("w3", [65, LAYERS, 65], f32)
        wroot = sb("wroot", [FEAT, FEAT], f32)
        wlast = sb("wlast", [ECAT, FEAT], f32)
        wpq = sb("wpq", [FEAT, 4 * FEAT], f32)
        bpq = sb("bpq", [1, 4 * FEAT], f32)
        ecat = sb("ecat", [P, TILES, ECAT], f32)
        wedge = sb("wedge", [EDGE_F, 2 * FEAT], f32)
        vecs = sb("vecs", [P, 3, FEAT], f32)
        bounds = sb("bounds", [P, 2 * PAIRS_PER_ROW], f32)
        tgrid = sb("tgrid", [P, 2, TILES], f32)
        pnum = sb("pnum", [P, 2, PAIRS_PER_ROW], f32)
        hit = sb("hit", [P, PAIRS_PER_ROW, 2, TILES], f32)
        ext = sb("ext", [2 * TILES, 1], f32)
        row = sb("row", [1, 5, TILES], f32)
        trip = sb("trip", [1, 3, TILES], i32)
        tmp_i = sb("tmp_i", [P, P], i32)
        bn = sb("bn", [P, 3, FEAT], f32)
        eps = sb("eps", [P, 1], f32)

        ps = ctx.enter_context(nc.psum_tensor("ps", [P, 8 * 512], f32))

        def bank(b, n=512):
            return ps[:, 512 * b:512 * b + n]

        adj_acc = ps[:, 0:NPAD]
        last_acc = ps[:, 7 * 512:7 * 512 + 1]

        s_const = sem("s_const"); s_const_v = sem("s_const_v"); s_w = sem("s_w"); s_in = sem("s_in")
        s_wz = sem("s_wz")
        s_ch = sem("s_ch")
        s_drow = [sem(f"s_drow{b}") for b in range(2)]; s_drow_free = sem("s_drow_free")
        s_pair = sem("s_pair"); s_hit = sem("s_hit"); s_hitT = sem("s_hitT"); s_ext = sem("s_ext")
        s_extT = sem("s_extT"); s_trip = sem("s_trip"); s_ready = sem("s_ready")
        s_oh = sem("s_oh"); s_chunk = sem("s_chunk"); s_tile = sem("s_tile"); s_merge = sem("s_merge"); s_lastz = sem("s_lastz")
        s_adj_v = sem("s_adj_v"); s_adj_a = sem("s_adj_a")
        s_x = sem("s_x"); s_gat = sem("s_gat"); s_e16 = sem("s_e16")
        s_var = sem("s_var"); s_std = sem("s_std"); s_y = sem("s_y"); s_agg = sem("s_agg")
        s_t12 = sem("s_t12"); s_t3 = sem("s_t3"); s_proj = sem("s_proj"); s_used = sem("s_used")
        s_cat = sem("s_cat"); s_catT = sem("s_catT"); s_catS = sem("s_catS"); s_catO = sem("s_catO")
        s_catU = sem("s_catU")
        s_pq = [sem(f"s_pq{b}") for b in range(2)]; s_io3 = sem("s_io3"); s_idx3 = sem("s_idx3"); s_in3 = sem("s_in3")
        s_et = [sem(f"s_et{b}") for b in range(2)]; s_g = [sem(f"s_g{b}") for b in range(2)]
        s_z = sem("s_z"); s_add1 = sem("s_add1"); s_add = sem("s_add"); s_en = sem("s_en"); s_ab = sem("s_ab")
        s_e2 = sem("s_e2"); s_ln = sem("s_ln"); s_one = sem("s_one"); s_rcp = sem("s_rcp"); s_mx = sem("s_mx")
        s_hm = sem("s_hm"); s_m1 = sem("s_m1"); s_r1 = sem("s_r1"); s_m2 = sem("s_m2"); s_m3 = sem("s_m3")
        s_oh3 = sem("s_oh3"); s_sc = sem("s_sc"); s_now = sem("s_now"); s_go = sem("s_go"); s_z3 = sem("s_z3");
        s_msg = sem("s_msg"); s_sum = sem("s_sum"); s_sq = sem("s_sq"); s_sqs = sem("s_sqs")
        s_bnv = sem("s_bnv"); s_bns = sem("s_bns"); s_fin = sem("s_fin"); s_out = sem("s_out")

        block = ctx.enter_context(nc.Block())

        def tile_trip(eng, t):
            first = eng.value_load(trip[0:1, 0, ds(t, 1)], min_val=0, max_val=PAIRS - 1)
            count = eng.value_load(trip[0:1, 1, ds(t, 1)], min_val=1, max_val=PAIRS)
            before = eng.value_load(trip[0:1, 2, ds(t, 1)], min_val=0, max_val=PAIRS * TILES)
            return first, count, before

        def chunk_of(first, j, a):
            c = nc.s_assert_within((first + j) * 2 + a, 0, CHUNKS - 1,
                                   skip_runtime_bounds_check_because="a tile's pairs end at its last pair")
            return ds(c, 1)

        n_weights = 0

        @block.sync
        def _(sp):
            nonlocal n_weights
            sp.dma_start(S["dst_i"], dst_cols).then_inc(s_in, 16)
            sp.dma_start(S["src_i"], src_cols).then_inc(s_in, 16)
            sp.dma_start(S["pair_dst"][0:PAIR_ROWS, :],
                         dst_rows.rearrange("(r q) e -> r (q e)", r=PAIR_ROWS)).then_inc(s_pair, 16)
            dflat = dst_rows.rearrange("c e -> (c e)")
            with sp.Fori(0, QUADS // 2) as i:
                for b in range(2):
                    sp.wait_ge(s_drow_free, 2 * i + b + 1)
                    sp.dma_start(S["drow"][:, 512 * b:512 * (b + 1)],
                                 dflat[ds(i * 1024 + 512 * b, 512)].partition_broadcast(P)).then_inc(s_drow[b], 16)
            sp.wait_ge(s_wz, 1)
            w_list = [sage_wl, gcn_w] + [mean_wt[64 * l:64 * (l + 1), :] for l in range(3)]
            moves = []
            for l, w in enumerate(w_list):
                moves += [(w12[0:64, l, 0:64], w), (w12[64:128, l, 0:64], w), (w3[0:64, l, 0:64], w)]
            moves += [(wroot[:, :], sage_wr), (wlast[0:16, :], sage_we), (wlast[16:17, :], sage_be),
                      (wlast[17:18, :], sage_bl)]
            for k, (w, b_row) in enumerate(((wf, bf_), (ws, bs_))):
                moves += [(wpq[0:64, 64 * k:64 * (k + 1)], w[0:64, :]),
                          (wpq[0:64, 128 + 64 * k:128 + 64 * (k + 1)], w[64:128, :]),
                          (bpq[:, 128 + 64 * k:128 + 64 * (k + 1)], b_row),
                          (wedge[:, 64 * k:64 * (k + 1)], w[128:160, :])]
            for k, v in enumerate((gcn_b, gamma, beta)):
                moves.append((vecs[:, k, :], v.rearrange("o f -> (o f)").partition_broadcast(P)))
            for to, of in moves:
                sp.dma_start(to, of).then_inc(s_w, 16)
            n_weights = len(moves)
            sp.wait_ge(s_adj_v, TILES + 1)
            sp.wait_ge(s_adj_a, TILES + 1)
            sp.dma_start(xs, x.rearrange("(t p) f -> p t f", p=P)).then_inc(s_x, 16)
            for t in range(TILES):
                sp.wait_ge(s_catU, GROUPS + t + 1)
                b = t % 2
                v = M["pq"][:, 256 * b:256 * (b + 1)]
                sp.dma_start(table_p[P * t:P * (t + 1), :], v[:, 0:128]).then_inc(s_pq[b], 16)
                sp.dma_start(table_q[P * t:P * (t + 1), :], v[:, 128:256]).then_inc(s_pq[b], 16)
            sp.dma_start(M["src_i"], src_cols).then_inc(s_in3, 16)
            sp.dma_start(M["dst_i"], dst_cols).then_inc(s_in3, 16)
            with sp.Fori(0, QUADS // 2) as i:
                for b in range(2):
                    sp.wait_ge(s_z, 2 * i + b + 1)
                    sp.dma_start(M["e_t"][0:EDGE_F, 512 * b:512 * (b + 1)],
                                 e32t[:, ds(i * 1024 + 512 * b, 512)]).then_inc(s_et[b], 16)
            sp.wait_ge(s_fin, 1)
            full = (TILES - 1) * P
            sp.dma_start(out[0:full, :].rearrange("(t p) f -> p t f", p=P), xs[:, 0:TILES - 1, :]).then_inc(s_out, 16)
            sp.dma_start(out[full:N_NODES, :], xs[0:LAST, TILES - 1, :]).then_inc(s_out, 16)
            sp.wait_ge(s_out, 32)

        @block.gpsimd
        def _(pool):
            g = nc.gpsimd
            g.iota(B["node_iota"], pattern=[[1, NPAD]], base=0, channel_multiplier=0)
            idv = S["ids_i"].rearrange("p (c k) -> p c k", k=3)
            g.iota(idv[:, :, 0], pattern=[[512, QUADS], [0, 4]], base=0, channel_multiplier=0)
            g.iota(idv[:, :, 1], pattern=[[0, QUADS], [128, 4]], base=0, channel_multiplier=0)
            g.iota(idv[:, :, 2], pattern=[[0, CHUNKS]], base=1, channel_multiplier=1)
            g.iota(tmp_i[:], pattern=[[1, P]], base=0, channel_multiplier=-1).then_inc(s_const, 1)
            pool.wait_ge(s_const_v, 1)
            g.iota(tmp_i[:, 0:25], pattern=[[P, TILES]], base=0, channel_multiplier=0)
            g.iota(tmp_i[:, 25:50], pattern=[[P, TILES]], base=P, channel_multiplier=0)
            g.iota(tmp_i[:, 50:54], pattern=[[1, 4]], base=1, channel_multiplier=4)
            g.iota(tmp_i[:, 54:58], pattern=[[-1, 4]], base=PAIRS, channel_multiplier=-4).then_inc(s_const, 1)
            pool.wait_ge(s_gat, 1)
            for t in range(TILES):
                g.indirect_dma_start(out=ecat[:, t, 0:EDGE_D], out_offset=None, in_=e16,
                                     in_offset=bass.IndirectOffsetOnAxis(ap=gat_i[:, t:t + 1], axis=0)
                                     ).then_inc(s_e16, 16)
            pool.wait_ge(s_used, LAYERS * GROUPS + 2)
            g.iota(M["node_iota"], pattern=[[1, NPAD]], base=0, channel_multiplier=0).then_inc(s_io3, 1)
            pool.wait_ge(s_idx3, 1)
            for b in range(2):
                pool.wait_ge(s_pq[b], 32 * ((TILES + 1 - b) // 2))
            with pool.Fori(0, QUADS // 2) as i:
                for b in range(2):
                    pool.wait_ge(s_add, 2 * i + b + 1)
                    now = M["now"][:, 8 * b:8 * b + 8]
                    g.tensor_copy(now[:, 0:4], M["src_i"][:, ds(i * 8 + 4 * b, 4)])
                    g.tensor_copy(now[:, 4:8], M["dst_i"][:, ds(i * 8 + 4 * b, 4)]).then_inc(s_now, 1)
                    pool.wait_ge(s_now, 2 * i + b + 1)
                    pool.sem_inc(s_go, 1)
                    for c in range(4):
                        o = 512 * b + 128 * c
                        g.indirect_dma_start(out=M["gp"][:, o:o + 128], out_offset=None, in_=table_p,
                                             in_offset=bass.IndirectOffsetOnAxis(ap=now[:, c:c + 1], axis=0)
                                             ).then_inc(s_g[b], 16)
                        g.indirect_dma_start(out=M["gq"][:, o:o + 128], out_offset=None, in_=table_q,
                                             in_offset=bass.IndirectOffsetOnAxis(ap=now[:, 4 + c:5 + c], axis=0)
                                             ).then_inc(s_g[b], 16)

        @block.vector
        def _(v):
            dve = nc.vector
            chain = [0]

            def link(ins):
                chain[0] += 1
                ins.then_inc(s_ch, 1)
                v.wait_ge(s_ch, chain[0])

            dve.memset(w12[:], 0.0)
            dve.memset(bpq[:], 0.0)
            link(dve.memset(w3[:], 0.0))
            dve.memset(w3[64:65, :, 64:65], 1.0).then_inc(s_wz, 1)
            dve.memset(ones[:], 1.0)
            dve.memset(eps[:], 1e-5)
            dve.memset(last_id[:], 0.0)
            dve.memset(B["zeros"], 0.0)
            v.wait_ge(s_const, 1)
            dve.tensor_scalar(ident[:], tmp_i[:], 0.0, None, ALU.is_equal)
            dve.tensor_scalar(ident16[:], tmp_i[:], 0.0, None, ALU.is_equal)
            dve.tensor_copy(S["ids"], S["ids_i"])
            dve.tensor_scalar(after[:], tmp_i[:], 0.0, None, ALU.is_gt).then_inc(s_const_v, 1)
            v.wait_ge(s_in, 32)
            dve.tensor_copy(B["srcf"], S["src_i"])
            link(dve.tensor_copy(B["dstf"], S["dst_i"]))
            v.wait_ge(s_const, 2)
            dve.tensor_copy(tgrid[:, :, :], tmp_i[:, 0:50].rearrange("p (a t) -> p a t", a=2))
            dve.tensor_copy(pnum[:, :, :], tmp_i[:, 50:58].rearrange("p (a t) -> p a t", a=2))
            v.wait_ge(s_pair, 16)
            pd = S["pair_dst"][0:PAIR_ROWS, :].rearrange("p (q e) -> p q e", q=PAIRS_PER_ROW)
            dve.tensor_reduce(bounds[0:PAIR_ROWS, 0:4], pd, AX.X, ALU.min)
            link(dve.tensor_reduce(bounds[0:PAIR_ROWS, 4:8], pd, AX.X, ALU.max))
            r = slice(0, PAIR_ROWS)
            for q in range(PAIRS_PER_ROW):
                link(dve.tensor_scalar(hit[r, q, 0, :], tgrid[r, 0, :], bounds[r, 4 + q:5 + q], None, ALU.is_le))
                link(dve.scalar_tensor_tensor(hit[r, q, 0, :], tgrid[r, 1, :], bounds[r, q:q + 1], hit[r, q, 0, :],
                                              ALU.is_gt, ALU.mult))
                dve.tensor_scalar(hit[r, q, 1, :], hit[r, q, 0, :], pnum[r, 0, q:q + 1], None, ALU.mult).then_inc(s_ch, 1)
                chain[0] += 1
                v.wait_ge(s_ch, chain[0])
                link(dve.tensor_scalar(hit[r, q, 0, :], hit[r, q, 0, :], pnum[r, 1, q:q + 1], None, ALU.mult))
            dve.memset(row[:, 4, :], 0.0).then_inc(s_hit, 1)
            v.wait_ge(s_hitT, 1)
            dve.tensor_reduce(ext[:, :], ps[0:2 * TILES, 0:PAIR_ROWS * 4], AX.X, ALU.max).then_inc(s_ext, 1)
            v.wait_ge(s_extT, 1)
            er = ps[0:1, 512:512 + 2 * TILES]
            link(dve.tensor_scalar(row[:, 0, :], er[:, 0:TILES], -1.0, float(PAIRS), ALU.mult, ALU.add))
            link(dve.tensor_scalar(row[:, 0, :], row[:, 0, :], float(PAIRS - 1), None, ALU.min))
            link(dve.tensor_tensor(row[:, 1, :], er[:, TILES:2 * TILES], row[:, 0, :], ALU.subtract))
            link(dve.tensor_scalar(row[:, 1, :], row[:, 1, :], 1.0, None, ALU.max))
            link(dve.tensor_tensor_scan(row[:, 2, :], row[:, 1, :], row[:, 4, :], 0.0, ALU.add, ALU.add))
            link(dve.tensor_tensor(row[:, 3, :], row[:, 2, :], row[:, 1, :], ALU.subtract))
            dve.tensor_copy(trip[:, 0:2, :], row[:, 0:2, :])
            link(dve.tensor_copy(trip[:, 2, :], row[:, 3, :]))
            v.sem_inc(s_drow_free, 2)
            with v.Fori(0, QUADS // 2) as i:
                for b in range(2):
                    v.wait_ge(s_drow[b], i * 16 + 16)
                    for c in range(4):
                        col = ds(i * 8 + (4 * b + c), 1)
                        ins = dve.scalar_tensor_tensor(
                            S["junk"][:, 128 * (c % 2):128 * (c % 2) + 128],
                            S["drow"][:, 512 * b + 128 * c:512 * b + 128 * c + 128], B["dstf"][:, col], after[:],
                            ALU.is_equal, ALU.mult, accum_out=B["later"][:, col])
                        ins.then_inc(s_merge, 1)
                        v.wait_ge(s_merge, i * 8 + (4 * b + c + 1))
                    v.sem_inc(s_drow_free, 1)
            m0 = CHUNKS
            link(dve.tensor_scalar(B["later"], B["later"], 0.0, None, ALU.is_equal))
            link(dve.tensor_tensor(flag_ids, S["ids"].rearrange("p (c k) -> p c k", k=3),
                                   B["later"].unsqueeze(2).broadcast_to([P, CHUNKS, 3]), ALU.mult))
            dve.memset(last_acc, 0.0).then_inc(s_lastz, 1)
            v.wait_ge(s_lastz, 1)
            v.sem_inc(s_adj_v, 1)
            v.sem_inc(s_ready, 1)

            def merge(t, wait_for):
                v.wait_ge(s_merge, wait_for)
                dve.tensor_tensor(last_id[:, ds(t, 1)], last_id[:, ds(t, 1)], last_acc,
                                  ALU.max).then_inc(s_merge, 1)

            with v.Fori(0, TILES) as t:
                first, count, before = tile_trip(v, t)
                with v.Fori(0, count) as j:
                    for a in range(2):
                        v.wait_ge(s_chunk, (before + j) * 2 + (a + 1))
                        merge(t, (before + j) * 2 + t * 2 + (m0 + a))
                        col = chunk_of(first, j, a)
                        dve.tensor_scalar(oh_src[:, a, :], B["node_iota"], B["srcf"][:, col], None, ALU.is_equal)
                        dve.tensor_scalar(oh_dst[:, a, :], B["node_iota"][:, ds(t * P, P)], B["dstf"][:, col],
                                          None, ALU.is_equal).then_inc(s_oh, 1)
                for a in range(2):
                    v.wait_ge(s_chunk, (before + count) * 2 + (a + 1))
                    merge(t, (before + count) * 2 + t * 2 + (m0 + a))
                v.wait_ge(s_merge, (before + count) * 2 + t * 2 + (m0 + 2))
                dve.memset(last_acc, 0.0).then_inc(s_lastz, 1)
                v.wait_ge(s_lastz, t + 2)
                v.wait_ge(s_tile, t + 1)
                dve.tensor_copy(A3[:, 16:TILES, ds(t * P, P)],
                                ps[:, 2048:NPAD].rearrange("p (k d) -> p k d", d=P)).then_inc(s_adj_v, 1)

            v.wait_ge(s_adj_v, TILES + 1)
            v.wait_ge(s_adj_a, TILES + 1)
            v.wait_ge(s_w, 16 * n_weights)
            link(dve.tensor_scalar(stat[:, 0, :], last_id[:], -1.0, 0.0, ALU.add, ALU.max))
            dve.tensor_copy(gat_i[:], stat[:, 0, :]).then_inc(s_gat, 1)
            link(dve.tensor_scalar(stat[:, 1, :], last_id[:], 0.0, None, ALU.is_gt))
            dve.memset(ecat[:, :, EDGE_D + 1:ECAT], 1.0)
            link(dve.tensor_copy(ecat[:, :, EDGE_D], stat[:, 1, :]))
            v.wait_ge(s_x, 16)

            wide = [P, TILES, FEAT]

            def over(s):
                return s.unsqueeze(2).broadcast_to(wide)

            n_std = [0]

            def layernorm_relu():
                link(dve.tensor_reduce(stat[:, 0, :], xs, AX.X, ALU.add))
                link(dve.tensor_scalar(stat[:, 0, :], stat[:, 0, :], -1.0 / FEAT, None, ALU.mult))
                link(dve.tensor_tensor(hs, xs, over(stat[:, 0, :]), ALU.add))
                link(dve.tensor_tensor(ts, hs, hs, ALU.mult))
                link(dve.tensor_reduce(stat[:, 1, :], ts, AX.X, ALU.add))
                dve.tensor_scalar(stat[:, 1, :], stat[:, 1, :], 1.0 / FEAT, 1e-5, ALU.mult, ALU.add).then_inc(s_var, 1)
                n_std[0] += 1
                v.wait_ge(s_std, n_std[0])
                link(dve.reciprocal(stat[:, 2, :], stat[:, 2, :]))
                link(dve.tensor_tensor(hs, hs, over(stat[:, 2, :]), ALU.mult))
                link(dve.tensor_scalar(hs, hs, 0.0, None, ALU.max))

            def split_y(y, l):
                link(dve.tensor_copy(y12[:, :, 0:FEAT], y))
                link(dve.tensor_tensor(ts, y, y12[:, :, 0:FEAT], ALU.subtract))
                link(dve.tensor_copy(y12[:, :, FEAT:2 * FEAT], ts))
                dve.tensor_tensor(y3[:, :, 0:FEAT], ts, y12[:, :, FEAT:2 * FEAT], ALU.subtract).then_inc(s_y, 1)

            link(dve.memset(y3[:, :, FEAT:FEAT + 2], 1.0))
            ps3 = [bank(2), bank(3)]
            po = [bank(4), bank(5)]
            for l in range(LAYERS):
                if l in (0, 1, 2):
                    layernorm_relu()
                if l == 0:
                    split_y(hs, l)
                elif l == 1:
                    link(dve.tensor_tensor(ts, hs, over(scale[:, 1, :]), ALU.mult))
                    split_y(ts, l)
                elif l == 2:
                    split_y(hs, l)
                else:
                    split_y(ts, l)
                for g in range(GROUPS):
                    b, n = g % 2, min(4, TILES - 4 * g)
                    G = GROUPS * l + g
                    v.wait_ge(s_agg, G + 1)
                    if G >= 2:
                        v.wait_ge(s_proj, G - 1)
                    dve.tensor_copy(t3[0:65, b, 0:P * n], ps3[b][0:65, 0:P * n]).then_inc(s_t3, 1)
                    v.wait_ge(s_proj, G + 1)
                    o = po[b].rearrange("p (t w) -> p t w", w=P)
                    tt = slice(4 * g, 4 * g + n)
                    sc = scale[:, min(l, 2), tt]
                    if l == 0:
                        link(dve.tensor_copy(cnt[:, tt], o[:, 0:n, 64]))
                        link(dve.tensor_scalar(scale[:, 0, tt], cnt[:, tt], 1.0, None, ALU.max))
                        link(dve.reciprocal(scale[:, 0, tt], scale[:, 0, tt]))
                    dve.tensor_tensor(ts[:, tt, :], o[:, 0:n, 0:FEAT], sc.unsqueeze(2).broadcast_to([P, n, FEAT]),
                                      ALU.mult).then_inc(s_used, 1)
                v.wait_ge(s_used, GROUPS * (l + 1) + 2)
                if l == 0:
                    v.wait_ge(s_e16, 16 * TILES)
                    dve.tensor_tensor(ecat[:, :, 0:EDGE_D], ecat[:, :, 0:EDGE_D],
                                      ecat[:, :, EDGE_D:EDGE_D + 1].broadcast_to([P, TILES, EDGE_D]),
                                      ALU.mult).then_inc(s_cat, 1)
                    d24 = adj[:, 0:(TILES - 1) * (NPAD + P)].rearrange("p (k d) -> p k d", k=TILES - 1)[:, :, 0:P]
                    link(dve.tensor_tensor(d24, d24, ident16[:, :].unsqueeze(1).broadcast_to([P, TILES - 1, P]), ALU.add))
                    dl = A3[:, TILES - 1, NPAD - P:NPAD]
                    link(dve.tensor_tensor(dl, dl, ident16[:, :], ALU.add))
                    link(dve.tensor_scalar(scale[:, 2, :], cnt[:, :], 1.0, None, ALU.add))
                    link(dve.reciprocal(scale[:, 2, :], scale[:, 2, :]))
                    dve.tensor_copy(stat[:, 1, :], scale[:, 2, :]).then_inc(s_var, 1)
                    n_std[0] += 1
                    v.wait_ge(s_std, n_std[0])
                    link(dve.tensor_copy(scale[:, 1, :], stat[:, 2, :]))
                    link(dve.tensor_tensor(xs, xs, ts, ALU.add))
                    for g in range(GROUPS):
                        n = min(4, TILES - 4 * g)
                        v.wait_ge(s_catO, g + 1)
                        dve.tensor_tensor(xs[:, 4 * g:4 * g + n, :], xs[:, 4 * g:4 * g + n, :],
                                          bank(0, FEAT * n).rearrange("p (t f) -> p t f", f=FEAT),
                                          ALU.add).then_inc(s_catU, 1)
                    v.wait_ge(s_catU, GROUPS)
                elif l == 1:
                    link(dve.tensor_tensor(xs, xs, ts, ALU.add))
                    link(dve.tensor_tensor(xs, xs, vecs[:, 0:1, :].broadcast_to(wide), ALU.add))
                elif l == 4:
                    link(dve.tensor_tensor(xs, xs, ts, ALU.add))
            layernorm_relu()
            v.sem_inc(s_cat, 1)
            for t in range(TILES):
                b = t % 2
                v.wait_ge(s_catO, GROUPS + t + 1)
                if t >= 2:
                    v.wait_ge(s_pq[b], 32 * (t // 2))
                dve.tensor_copy(M["pq"][:, 256 * b:256 * (b + 1)], bank(b, 256)).then_inc(s_catU, 1)
            v.wait_ge(s_in3, 32)
            v.wait_ge(s_io3, 1)
            link(dve.tensor_copy(M["srcf"], M["src_i"]))
            link(dve.memset(M["zeros"], 0.0))
            link(dve.tensor_scalar(M["dst_i"], M["dst_i"], float(N_NODES - 1), None, ALU.min))
            dve.tensor_scalar(M["src_i"], M["src_i"], float(N_NODES - 1), None, ALU.min).then_inc(s_idx3, 1)
            v.sem_inc(s_add, 2)
            v.wait_ge(s_idx3, 1)
            with v.Fori(0, QUADS // 2) as i:
                for b in range(2):
                    q = i * 2 + b

                    def half(name, lo=0, n=256):
                        return M[name][:, n * b + lo:n * b + lo + n]

                    def one_hot(c):
                        slot = 4 * b + c
                        v.wait_ge(s_sc, i * 8 + (4 * b + c + 1))
                        dve.tensor_scalar(M["oh"][:, slot * NPAD:(slot + 1) * NPAD], M["node_iota"],
                                          M["srcf"][:, ds(i * 8 + 4 * b + c, 1)], None,
                                          ALU.is_equal).then_inc(s_oh3, 1)

                    zb = M["z"][:, 512 * b:512 * (b + 1)]
                    v.wait_ge(s_z, q + 3)
                    v.wait_ge(s_g[b], i * 128 + 128)
                    dve.tensor_tensor(zb, M["gp"][:, 512 * b:512 * (b + 1)], bank(4 + b), ALU.add).then_inc(s_add1, 1)
                    v.wait_ge(s_add1, q + 1)
                    dve.tensor_tensor(zb, zb, M["gq"][:, 512 * b:512 * (b + 1)], ALU.add).then_inc(s_add, 1)
                    one_hot(0)
                    one_hot(1)
                    z3 = zb.rearrange("p (c w) -> p c w", w=P)
                    en, ab, ln, hm = (half(k).rearrange("p (c w) -> p c w", w=FEAT) for k in ("en", "ab", "ln", "hm"))
                    v.wait_ge(s_en, q + 1)
                    dve.tensor_scalar(en, en, 1.0, None, ALU.add).then_inc(s_one, 1)
                    v.wait_ge(s_ln, q + 1)
                    dve.scalar_tensor_tensor(ln, z3[:, :, FEAT:P], 0.0, ln, ALU.max, ALU.add).then_inc(s_mx, 1)
                    v.wait_ge(s_one, q + 1)
                    dve.reciprocal(en, en).then_inc(s_rcp, 1)
                    v.wait_ge(s_mx, q + 1)
                    v.wait_ge(s_rcp, q + 1)
                    dve.tensor_tensor(hm, en, ln, ALU.mult).then_inc(s_hm, 1)
                    one_hot(2)
                    m1 = M["m1"][:, 256 * b:256 * (b + 1)]
                    m2 = M["m2"][:, 256 * b:256 * (b + 1)]
                    m3 = M["m3"][:, 256 * b:256 * (b + 1)]
                    v.wait_ge(s_m1, q + 1)
                    dve.tensor_tensor(half("hm"), half("hm"), m1, ALU.subtract).then_inc(s_r1, 1)
                    one_hot(3)
                    v.wait_ge(s_m2, q + 1)
                    dve.tensor_tensor(m3, half("hm"), m2, ALU.subtract).then_inc(s_m3, 1)
            link(dve.tensor_tensor(xs, xs, hs, ALU.add))
            v.wait_ge(s_tile, TILES + 1)
            msg = M["msg"].rearrange("p (t f) -> p t f", f=FEAT)
            dve.tensor_copy(M["msg"], ps[:, 0:TILES * FEAT]).then_inc(s_msg, 1)
            v.wait_ge(s_sum, 1)
            link(dve.tensor_scalar(bn[:, 0, :], bank(6, FEAT), -1.0 / N_NODES, None, ALU.mult))
            link(dve.tensor_tensor(msg, msg, bn[:, 0:1, :].broadcast_to(wide), ALU.add))
            dve.tensor_tensor(ts, msg, msg, ALU.mult).then_inc(s_sq, 1)
            v.wait_ge(s_sqs, 1)
            dve.tensor_scalar(bn[:, 1, :], bank(7, FEAT), 1.0 / N_NODES, 1e-5, ALU.mult, ALU.add).then_inc(s_bnv, 1)
            v.wait_ge(s_bns, 1)
            link(dve.reciprocal(bn[:, 2, :], bn[:, 2, :]))
            link(dve.tensor_tensor(bn[:, 2, :], bn[:, 2, :], vecs[:, 1, :], ALU.mult))
            link(dve.tensor_tensor(msg, msg, bn[:, 2:3, :].broadcast_to(wide), ALU.mult))
            link(dve.tensor_tensor(msg, msg, vecs[:, 2:3, :].broadcast_to(wide), ALU.add))
            dve.tensor_tensor(xs, xs, msg, ALU.add).then_inc(s_fin, 1)

        @block.scalar
        def _(act):
            a = nc.scalar
            a.preload_act_table(ACT.Sqrt)
            act.wait_ge(s_ready, 1)
            act.sem_inc(s_adj_a, 1)
            with act.Fori(0, TILES) as t:
                act.wait_ge(s_tile, t + 1)
                a.copy(A3[:, 0:16, ds(t * P, P)],
                       ps[:, 0:2048].rearrange("p (k d) -> p k d", d=P)).then_inc(s_adj_a, 1)
            n_var = [0]

            def root():
                n_var[0] += 1
                act.wait_ge(s_var, n_var[0])
                a.activation(stat[:, 2, :], stat[:, 1, :], ACT.Sqrt).then_inc(s_std, 1)

            def cat_group(at, with_last):
                g = at % GROUPS
                b, n = g % 2, min(4, TILES - 4 * g)
                act.wait_ge(s_catT, at + 1)
                if with_last:
                    a.copy(t3[0:ECAT, b, 0:P * n], bank(7)[0:ECAT, 0:P * n])
                a.copy(t12[0:FEAT, b, 0:P * n], bank(6)[0:FEAT, 0:P * n]).then_inc(s_catS, 1)

            for l in range(LAYERS):
                if l < 3:
                    root()
                for g in range(GROUPS):
                    b, n = g % 2, min(4, TILES - 4 * g)
                    G = GROUPS * l + g
                    act.wait_ge(s_agg, G + 1)
                    if G >= 2:
                        act.wait_ge(s_proj, G - 1)
                    a.copy(t12[:, b, 0:P * n], bank(b, P * n)).then_inc(s_t12, 1)
                if l == 0:
                    root()
                    for g in range(GROUPS):
                        cat_group(g, True)
            root()
            for g in range(GROUPS):
                cat_group(GROUPS + g, False)
            a.preload_act_table_set("natural_log_exp_and_others")
            with act.Fori(0, QUADS // 2) as i:
                for b in range(2):
                    q = i * 2 + b

                    def half(name):
                        return M[name][:, 256 * b:256 * (b + 1)].rearrange("p (c w) -> p c w", w=FEAT)

                    z3 = M["z"][:, 512 * b:512 * (b + 1)].rearrange("p (c w) -> p c w", w=P)
                    act.wait_ge(s_add, q + 3)
                    a.activation(half("en"), z3[:, :, 0:FEAT], ACT.Exp, scale=-1.0).then_inc(s_en, 1)
                    a.activation(half("ab"), z3[:, :, FEAT:P], ACT.Abs).then_inc(s_ab, 1)
                    act.wait_ge(s_ab, q + 1)
                    a.activation(half("ab"), half("ab"), ACT.Exp, scale=-1.0).then_inc(s_e2, 1)
                    act.wait_ge(s_e2, q + 1)
                    a.activation(half("ln"), half("ab"), ACT.Ln, bias=1.0).then_inc(s_ln, 1)
                    act.wait_ge(s_hm, q + 1)
                    act.wait_ge(s_sc, q * 4 + 4)
                    a.copy(M["m1"][:, 256 * b:256 * (b + 1)], M["hm"][:, 256 * b:256 * (b + 1)]).then_inc(s_m1, 1)
                    act.wait_ge(s_r1, q + 1)
                    a.copy(M["m2"][:, 256 * b:256 * (b + 1)], M["hm"][:, 256 * b:256 * (b + 1)]).then_inc(s_m2, 1)
            act.wait_ge(s_bnv, 1)
            a.activation(bn[:, 2, :], bn[:, 1, :], ACT.Sqrt).then_inc(s_bns, 1)

        @block.tensor
        def _(pe):
            mm = nc.tensor.matmul
            pe.wait_ge(s_hit, 1)
            r = slice(0, PAIR_ROWS)
            for q in range(PAIRS_PER_ROW):
                last = mm(ps[0:2 * TILES, q * PAIR_ROWS:(q + 1) * PAIR_ROWS],
                          hit[r, q, :, :].rearrange("p a t -> p (a t)"), ident[r, 0:PAIR_ROWS], start=True, stop=True)
            last.then_inc(s_hitT, 1)
            pe.wait_ge(s_ext, 1)
            mm(ps[0:1, 512:512 + 2 * TILES], ext[:, :], ident[0:2 * TILES, 0:2 * TILES], start=True,
               stop=True).then_inc(s_extT, 1)
            pe.wait_ge(s_ready, 1)
            pe.wait_ge(s_const_v, 1)
            pe.sem_inc(s_chunk, 2)
            zl = B["zeros"][:, 0:P]
            zr = B["zeros"][:, 0:512]
            with pe.Fori(0, TILES) as t:
                first, count, before = tile_trip(pe, t)
                pe.wait_ge(s_adj_a, t + 1)
                pe.wait_ge(s_adj_v, t + 1)
                for k in range(7):
                    n = min(512, NPAD - 512 * k)
                    mm(bank(k, n), zl, zr[:, 0:n], start=True, stop=False)
                with pe.Fori(0, count) as j:
                    for a in range(2):
                        pe.wait_ge(s_oh, (before + j) * 2 + (a + 1))
                        for k in range(TILES):
                            mm(adj_acc[:, P * k:P * (k + 1)], oh_src[:, a, P * k:P * (k + 1)], oh_dst[:, a, :],
                               start=False, stop=False)
                        pe.wait_ge(s_merge, (before + j) * 2 + t * 2 + (CHUNKS + a + 2))
                        for k in range(3):
                            last = mm(last_acc, oh_dst[:, a, :],
                                      flag_ids[:, chunk_of(first, j, a), k], start=(k == 0), stop=(k == 2))
                        last.then_inc(s_chunk, 1)
                for k in range(7):
                    last = mm(ps[:, 512 * k:512 * k + 1], zl, zr[:, 0:1], start=False, stop=True)
                last.then_inc(s_tile, 1)

            def aggregate(l, g):
                b, n = g % 2, min(4, TILES - 4 * g) * P
                G = GROUPS * l + g
                if G >= 2:
                    pe.wait_ge(s_t12, G - 1)
                    pe.wait_ge(s_t3, G - 1)
                for k in range(TILES):
                    mm(bank(b, n), y12[:, k, :], A3[:, k, 512 * g:512 * g + n], start=(k == 0), stop=(k == TILES - 1))
                for k in range(TILES):
                    last = mm(bank(2 + b)[0:65, 0:n], y3[:, k, 0:65], A3[:, k, 512 * g:512 * g + n],
                              start=(k == 0), stop=(k == TILES - 1))
                last.then_inc(s_agg, 1)

            def project(l, g):
                b = g % 2
                G = GROUPS * l + g
                pe.wait_ge(s_t12, G + 1)
                pe.wait_ge(s_t3, G + 1)
                pe.wait_ge(s_used, G + 1)
                for i in range(min(4, TILES - 4 * g)):
                    o = ps[:, 512 * (4 + b) + P * i:512 * (4 + b) + P * i + 65]
                    mm(o, t12[:, b, P * i:P * (i + 1)], w12[:, l, :], start=True, stop=False)
                    last = mm(o, t3[0:65, b, P * i:P * (i + 1)], w3[:, l, :], start=False, stop=True)
                last.then_inc(s_proj, 1)

            def cat_group(at, with_last):
                g = at % GROUPS
                n = min(4, TILES - 4 * g)
                for i in range(n):
                    last = nc.tensor.transpose(bank(6)[0:FEAT, P * i:P * (i + 1)], hs[:, 4 * g + i, :], ident[:, :])
                    if with_last:
                        last = nc.tensor.transpose(bank(7)[0:ECAT, P * i:P * (i + 1)], ecat[:, 4 * g + i, :], ident[:, :])
                last.then_inc(s_catT, 1)
                pe.wait_ge(s_catS, at + 1)

            pe.wait_ge(s_w, 16 * n_weights)
            pe.sem_inc(s_used, 2)
            for l in range(LAYERS):
                pe.wait_ge(s_y, l + 1)
                if l == 1:
                    pe.wait_ge(s_catU, GROUPS)
                for g in range(GROUPS):
                    aggregate(l, g)
                    if g:
                        project(l, g - 1)
                project(l, GROUPS - 1)
                if l == 0:
                    pe.wait_ge(s_cat, 1)
                    for g in range(GROUPS):
                        b, n = g % 2, min(4, TILES - 4 * g)
                        cat_group(g, True)
                        if g:
                            pe.wait_ge(s_catU, g)
                        for i in range(n):
                            o = bank(0)[:, FEAT * i:FEAT * (i + 1)]
                            mm(o, t12[0:FEAT, b, P * i:P * (i + 1)], wroot[:, :], start=True, stop=False)
                            last = mm(o, t3[0:ECAT, b, P * i:P * (i + 1)], wlast[:, :], start=False, stop=True)
                        last.then_inc(s_catO, 1)
            pe.wait_ge(s_cat, 2)
            for g in range(GROUPS):
                b, n = g % 2, min(4, TILES - 4 * g)
                cat_group(GROUPS + g, False)
                for i in range(n):
                    t = 4 * g + i
                    if t >= 2:
                        pe.wait_ge(s_catU, GROUPS + t - 1)
                    o = bank(t % 2, 4 * FEAT)
                    mm(o, t12[0:FEAT, b, P * i:P * (i + 1)], wpq[:, :], start=True, stop=False)
                    mm(o, ones[0:1, :], bpq[:, :], start=False, stop=True).then_inc(s_catO, 1)
            pe.wait_ge(s_catU, GROUPS + TILES)
            pe.wait_ge(s_idx3, 1)
            for k in range(4):
                mm(bank(k), M["zeros"][:, 0:P], M["zeros"][:, 0:512], start=True, stop=False)
            pe.sem_inc(s_z, 2)
            pe.sem_inc(s_sc, SLOTS)

            def attributes(q, b, trips):
                pe.wait_ge(s_et[b], trips * 16 + 16)
                pe.wait_ge(s_add, q + 1)
                for c in range(4):
                    last = mm(ps[:, 512 * (4 + b) + P * c:512 * (4 + b) + P * (c + 1)],
                              M["e_t"][0:EDGE_F, 512 * b + P * c:512 * b + P * (c + 1)], wedge[:, :],
                              start=True, stop=True)
                last.then_inc(s_z, 1)

            def scatter(q, b):
                pe.wait_ge(s_m3, q + 1)
                for c in range(4):
                    pe.wait_ge(s_oh3, q * 4 + (c + 1))
                    row0 = (4 * b + c) * NPAD
                    for k in range(TILES):
                        for part in ("m1", "m2", "m3"):
                            last = mm(ps[:, FEAT * k:FEAT * (k + 1)], M["oh"][:, row0 + P * k:row0 + P * (k + 1)],
                                      M[part][:, 256 * b + FEAT * c:256 * b + FEAT * (c + 1)], start=False, stop=False)
                    last.then_inc(s_sc, 1)

            attributes(0, 0, 0)
            with pe.Fori(0, QUADS // 2 - 1) as i:
                attributes(i * 2 + 1, 1, i)
                scatter(i * 2, 0)
                attributes(i * 2 + 2, 0, i + 1)
                scatter(i * 2 + 1, 1)
            attributes(QUADS - 1, 1, QUADS // 2 - 1)
            scatter(QUADS - 2, 0)
            scatter(QUADS - 1, 1)
            for k in range(4):
                last = mm(ps[:, 512 * k:512 * k + 1], M["zeros"][:, 0:P], M["zeros"][:, 0:1], start=False, stop=True)
            last.then_inc(s_tile, 1)
            msg = M["msg"].rearrange("p (t f) -> p t f", f=FEAT)
            pe.wait_ge(s_msg, 1)
            for t in range(TILES):
                last = mm(bank(6, FEAT), ones[:, :], msg[:, t, :], start=(t == 0), stop=(t == TILES - 1))
            last.then_inc(s_sum, 1)
            pe.wait_ge(s_sq, 1)
            for t in range(TILES):
                rows = P if t < TILES - 1 else LAST
                last = mm(bank(7, FEAT), ones[0:rows, :], ts[0:rows, t, :], start=(t == 0), stop=(t == TILES - 1))
            last.then_inc(s_sqs, 1)


def kernel(x, src, dst, edge_attr_16, edge_attr_32, L0_gnn_W_l, L0_gnn_b_l, L0_gnn_W_r, L0_gnn_W_e, L0_gnn_b_e,
           L1_gnn_W, L1_gnn_b, L2_gnn_weights, L3_gnn_W_f, L3_gnn_b_f, L3_gnn_W_s, L3_gnn_b_s, L3_gnn_gamma,
           L3_gnn_beta):
    import numpy as np
    import concourse.bacc as bacc
    from concourse.bass_utils import run_bass_kernel_spmd

    def padded(a, size, value):
        a = np.asarray(a)
        wide = np.full((size,) + a.shape[1:], value, a.dtype)
        wide[:a.shape[0]] = a
        return wide

    src_rows = padded(src, CHUNKS * P, PAD).reshape(CHUNKS, P)
    dst_rows = padded(dst, CHUNKS * P, PAD).reshape(CHUNKS, P)
    row = lambda a: np.asarray(a).reshape(1, FEAT)
    w2 = np.asarray(L2_gnn_weights)
    arrays = {
        "x": padded(x, NPAD, 0),
        "src_cols": src_rows.T, "dst_cols": dst_rows.T, "dst_rows": dst_rows,
        "e16": edge_attr_16, "e32t": padded(edge_attr_32, CHUNKS * P, 0).T,
        "sage_wl": L0_gnn_W_l, "sage_bl": row(L0_gnn_b_l), "sage_wr": L0_gnn_W_r, "sage_we": L0_gnn_W_e,
        "sage_be": row(L0_gnn_b_e), "gcn_w": L1_gnn_W, "gcn_b": row(L1_gnn_b),
        "mean_wt": w2.transpose(0, 2, 1).reshape(3 * FEAT, FEAT),
        "wf": L3_gnn_W_f, "bf": row(L3_gnn_b_f), "ws": L3_gnn_W_s, "bs": row(L3_gnn_b_s),
        "gamma": row(L3_gnn_gamma), "beta": row(L3_gnn_beta),
    }
    arrays = {f"in_{k}": np.ascontiguousarray(a) for k, a in arrays.items()}
    nc = bacc.Bacc("TRN2", target_bir_lowering=False, num_devices=1)
    args = [nc.dram_tensor(k, a.shape, mybir.dt.from_np(a.dtype), kind="ExternalInput").ap()
            for k, a in arrays.items()]
    args.append(nc.dram_tensor("out_x", (N_NODES, FEAT), mybir.dt.float32, kind="ExternalOutput").ap())
    gnn_program(nc, *args)
    result = run_bass_kernel_spmd(nc, [arrays], core_ids=[0])
    return result.results[0]["out_x"]
```

```python
import concourse.bass as bass
from concourse import mybir
from concourse.bass import ds
from contextlib import ExitStack

N_NODES = 3125
FEAT = 64
N_EDGES = 103125
P = 128
TILES = -(-N_NODES // P)
NPAD = TILES * P
LAST = N_NODES - (TILES - 1) * P
CHUNKS = -(-N_EDGES // (8 * P)) * 8
PAIRS = CHUNKS // 2
QUADS = CHUNKS // 4
QPR = 2
QUAD_ROWS = QUADS // QPR
EDGE_F = 32
EDGE_D = 16
LAYERS = 5
GROUPS = -(-TILES // 4)
ECAT = EDGE_D + 2
PAD = 4095
WIN = 64
WINDOWS = NPAD // WIN
RUN = 10
MOV = TILES * WIN
BLOCK = 8
SPAN = 512
SPANS = (N_EDGES + TILES * (SPAN - 1)) // SPAN
TABLE = SPANS * SPAN
PAYLOAD = EDGE_F + 2
MOVED = -(-N_EDGES // P)
BATCH = 13
EARLY = 4
FILL = 8
ARENA = 18600


def gnn_program(nc, x, src_cols, dst_cols, dst_rows, e16, e32, sage_wl, sage_bl, sage_wr, sage_we,
                sage_be, gcn_w, gcn_b, mean_wt, wf, bf_, ws, bs_, gamma, beta, out):
    f32, bf16, i32, i16 = mybir.dt.float32, mybir.dt.bfloat16, mybir.dt.int32, mybir.dt.int16
    ALU, ACT, AX = mybir.AluOpType, mybir.ActivationFunctionType, mybir.AxisListType

    table_e = nc.dram_tensor("table_e", [TABLE + P, PAYLOAD], f32, kind="Internal").ap()
    table_q = nc.dram_tensor("table_q", [NPAD, 2 * FEAT], f32, kind="Internal").ap()

    with ExitStack() as ctx:
        def sb(name, shape, dt):
            return ctx.enter_context(nc.sbuf_tensor(name, shape, dt))

        def sem(name):
            return ctx.enter_context(nc.semaphore(name))

        adj = sb("adj", [P, TILES * NPAD], bf16)
        arena = sb("arena", [P, ARENA], bf16)
        A3 = adj[:, :].rearrange("p (k d) -> p k d", k=TILES)

        def views(base, wanted, limit):
            found, at = {}, 0
            for name, words, dt in wanted:
                v = base[:, at:at + 2 * words]
                found[name] = v if dt == bf16 else v.bitcast(dt)
                at += 2 * words
            assert at <= limit, at
            return found

        B = views(arena, [("iota", MOV // 2, i16), ("key_lo", CHUNKS, f32), ("key_mv", CHUNKS, f32),
                          ("oh_lo", 2 * P, bf16), ("oh_mv", 2 * MOV, bf16), ("edge_at", CHUNKS, i32),
                          ("ends", CHUNKS, i16), ("payload", 2 * BATCH * PAYLOAD, f32), ("moving", 2 * BATCH, i32),
                          ("wgrid", 3 * WINDOWS, f32), ("iota_f", P, f32),
                          ("lo_base", 2 * P, f32), ("lo_far", 2 * P, bf16)], ARENA)
        E = views(B["oh_mv"], [("tmp_i", P, i32), ("bounds", 8, f32), ("row", 5 * WINDOWS, f32),
                               ("fill", FILL * PAYLOAD, f32), ("before", P, f32)], 4 * MOV)
        tmp_i, bounds = E["tmp_i"], E["bounds"]
        row = E["row"][0:1, :].rearrange("p (k w) -> p k w", k=5)
        wgrid = B["wgrid"].rearrange("p (k w) -> p k w", k=3)
        payload = B["payload"].rearrange("p (b c w) -> p b c w", b=2, c=BATCH)
        ends = B["ends"].rearrange("p (c w) -> p c w", w=2)
        oh_lo = B["oh_lo"].rearrange("p (s n) -> p s n", s=4)
        oh_mv = B["oh_mv"].rearrange("p (s n) -> p s n", s=4)
        lo_far = B["lo_far"].rearrange("p (s n) -> p s n", s=4)
        S = views(adj, [("src_i", CHUNKS, i32), ("dst_i", CHUNKS, i32), ("ka", CHUNKS, i32), ("kb", CHUNKS, i32),
                        ("quad_dst", QPR * 512, i32), ("dlo", CHUNKS, f32), ("dhi", CHUNKS, i32),
                        ("oh_dhi", BLOCK * WINDOWS, bf16), ("oh_dlo", BLOCK * WIN, bf16), ("half_no", WINDOWS, i32),
                        ("seen", PAIRS * TILES // 2, bf16), ("seen_at", PAIRS * TILES, f32),
                        ("rows", TILES * 256, i32), ("pair_no", PAIRS, i32), ("edge_no", 256, i32),
                        ("node_no", TILES, i32), ("win_i", 3 * WINDOWS, i32),
                        ("hit", QPR * 2 * WINDOWS, f32)], TILES * NPAD)
        hit = S["hit"].rearrange("p (q a w) -> p q a w", q=QPR, a=2)
        R = views(S["seen"], [("tile_f", CHUNKS, f32), ("rank", CHUNKS, f32), ("mine", CHUNKS, f32),
                              ("at", CHUNKS, f32), ("counts", TILES, f32), ("spans", TILES, f32),
                              ("spans_i", TILES, i32), ("base", TILES, f32), ("upto", TILES, f32),
                              ("dump_i", 1, i32), ("dump", 1, f32)], PAIRS * TILES)
        oh_tile = S["seen_at"].bitcast(bf16).rearrange("p (t c) -> p t c", t=TILES)
        L = views(arena, [("x", TILES * FEAT, f32), ("h", TILES * FEAT, f32), ("t", TILES * FEAT, f32),
                          ("y12", TILES * FEAT, bf16), ("y3", TILES * 33, bf16),
                          ("t12", 1024, f32), ("t3", 1024, f32)], ARENA)
        xs, hs, ts = (L[k].rearrange("p (t f) -> p t f", f=FEAT) for k in ("x", "h", "t"))
        y12 = L["y12"].rearrange("p (t f) -> p t f", f=2 * FEAT)
        y3 = L["y3"].rearrange("p (t f) -> p t f", f=66)
        t12 = L["t12"].rearrange("p (s n) -> p s n", s=2)
        t3 = L["t3"].rearrange("p (s n) -> p s n", s=2)
        M = views(adj, [("p3", TILES * 3 * FEAT, bf16), ("pf", TILES * 2 * FEAT, f32), ("lane", P, f32),
                        ("lane_i", P, i32), ("pay", 4 * 4 * PAYLOAD, f32), ("now", 16, i32), ("gq", 2 * 512, f32),
                        ("oh", 4 * 256, bf16), ("oht", 2 * 256, bf16), ("et", 4 * P, f32), ("w_edge", 2 * P, f32), ("z", 2 * 512, f32),
                        ("ab", 2 * 512, f32), ("ln", 2 * 512, f32), ("gate", 2 * 256, f32), ("val", 2 * 256, f32),
                        ("hm", 256, f32), ("m1", 256, bf16), ("m2", 256, bf16), ("m3", 256, bf16),
                        ("msg", TILES * FEAT, f32), ("pq", 2 * 128, f32), ("zeros", 256, bf16),
                        ("span_no", SPANS, i32), ("is_upto", SPANS * TILES, f32), ("tile_f", SPANS, f32),
                        ("tile_of", SPANS, i32)], TILES * NPAD)

        w_edge = M["w_edge"][0:2 * PAYLOAD, :]
        ident = sb("ident", [P, P], f32)
        ident16 = sb("ident16", [P, P], bf16)
        zeros = sb("zeros", [P, P], bf16)
        ones = sb("ones", [P, P], f32)
        last_pair = sb("last_pair", [P, TILES], f32)
        cnt = sb("cnt", [P, TILES], f32)
        scale = sb("scale", [P, 3, TILES], f32)
        stat = sb("stat", [P, 3, TILES], f32)
        gat_i = sb("gat_i", [P, TILES], i32)
        gat_e = sb("gat_e", [P, TILES], i32)
        w12 = sb("w12", [P, LAYERS, 65], f32)
        w3 = sb("w3", [65, LAYERS, 65], f32)
        wroot = sb("wroot", [FEAT, FEAT], f32)
        wlast = sb("wlast", [ECAT, FEAT], f32)
        wpq = sb("wpq", [FEAT, 4 * FEAT], f32)
        bpq = sb("bpq", [1, 4 * FEAT], f32)
        ecat = sb("ecat", [P, TILES, ECAT], f32)
        vecs = sb("vecs", [P, 3, FEAT], f32)
        span0 = sb("span0", [P, TILES], f32)
        pnum = sb("pnum", [P, 2, QPR], f32)
        ext = sb("ext", [WINDOWS, 2], f32)
        trip = sb("trip", [1, 3, WINDOWS], i32)
        pnum_i = sb("pnum_i", [P, 2 * QPR], i32)
        bn = sb("bn", [P, 3, FEAT], f32)

        ps = ctx.enter_context(nc.psum_tensor("ps", [P, 8 * 512], f32))

        def bank(b, n=512):
            return ps[:, 512 * b:512 * b + n]

        adj_acc = [ps[:, 0:MOV], ps[:, 2048:2048 + MOV]]

        s_const = sem("s_const"); s_w = sem("s_w"); s_in = sem("s_in")
        s_wz = sem("s_wz")
        s_ch = sem("s_ch")
        s_pair = sem("s_pair"); s_hit = sem("s_hit"); s_hitT = sem("s_hitT"); s_ext = sem("s_ext")
        s_extT = sem("s_extT"); s_trip = sem("s_trip"); s_ready = sem("s_ready")
        s_oh = sem("s_oh"); s_lo = sem("s_lo"); s_base = sem("s_base"); s_far = sem("s_far"); s_chunk = sem("s_chunk"); s_tile = sem("s_tile"); 
        s_adj = sem("s_adj"); s_win = sem("s_win"); s_lp = sem("s_lp"); s_rows = sem("s_rows")
        s_seen_c = sem("s_seen_c"); s_seen_o = sem("s_seen_o"); s_seen_a = sem("s_seen_a")
        s_x = sem("s_x"); s_gat = sem("s_gat"); s_e16 = sem("s_e16")
        s_var = sem("s_var"); s_std = sem("s_std"); s_y = sem("s_y"); s_agg = sem("s_agg")
        s_t12 = sem("s_t12"); s_t3 = sem("s_t3"); s_proj = sem("s_proj"); s_used = sem("s_used")
        s_cat = sem("s_cat"); s_catT = sem("s_catT"); s_catS = sem("s_catS"); s_catO = sem("s_catO")
        s_catU = sem("s_catU")
        s_pq = [sem(f"s_pq{b}") for b in range(2)]; s_io3 = sem("s_io3"); s_p3 = sem("s_p3")
        s_fs = sem("s_fs"); s_fill = sem("s_fill"); s_tiles = sem("s_tiles"); s_counts = sem("s_counts")
        s_pre = sem("s_pre"); s_place = sem("s_place"); s_rank = sem("s_rank")
        s_e32 = [sem(f"s_e32_{b}") for b in range(2)]; s_moved = [sem(f"s_moved{b}") for b in range(2)]
        s_ids = sem("s_ids"); s_go = sem("s_go")
        s_pay = [sem(f"s_pay{b}") for b in range(4)]; s_now = sem("s_now"); s_g = [sem(f"s_g{b}") for b in range(2)]
        s_oh3 = sem("s_oh3"); s_tr = sem("s_tr"); s_ct = sem("s_ct"); s_z = sem("s_z"); s_add = sem("s_add")
        s_ab = sem("s_ab"); s_ex = sem("s_ex"); s_ln = sem("s_ln"); s_ga = sem("s_ga"); s_gt = sem("s_gt")
        s_hm = sem("s_hm"); s_m1 = sem("s_m1"); s_r1 = sem("s_r1"); s_m2 = sem("s_m2"); s_m3 = sem("s_m3")
        s_sc = sem("s_sc"); s_wb0 = sem("s_wb0"); s_wb = sem("s_wb")
        s_msg = sem("s_msg"); s_sum = sem("s_sum"); s_sq = sem("s_sq"); s_sqs = sem("s_sqs")
        s_bnv = sem("s_bnv"); s_bns = sem("s_bns"); s_fin = sem("s_fin"); s_out = sem("s_out")

        block = ctx.enter_context(nc.Block())

        def trip_value(eng, t, part):
            least, most = ((0, QUADS - 3), (3, QUADS), (0, QUADS * WINDOWS))[part]
            return eng.value_load(trip[0:1, part, ds(t, 1)], min_val=least, max_val=most)

        def window_trip(eng, t):
            return [trip_value(eng, t, part) for part in range(3)]

        def chunk_of(first, j, a):
            c = nc.s_assert_within((first + j) * 4 + a, 0, CHUNKS - 1,
                                   skip_runtime_bounds_check_because="a window's chunks end at the last chunk")
            return ds(c, 1)

        def pair_of(name, b, n):
            return M[name][:, n * b:n * (b + 1)]

        def pay(slot):
            return M["pay"][:, 4 * PAYLOAD * slot:4 * PAYLOAD * (slot + 1)]

        def pay_of(slot):
            return pay(slot).rearrange("p (c w) -> p c w", c=4)

        def msg_of(eng, i, k):
            return eng.value_load(M["tile_of"][0:1, ds(i * 4 + k, 1)], min_val=0, max_val=TILES - 1)

        n_weights = 0

        @block.sync
        def _(sp):
            nonlocal n_weights
            sp.dma_start(S["dst_i"], dst_cols).then_inc(s_in, 16)
            sp.dma_start(S["src_i"], src_cols).then_inc(s_in, 16)
            sp.dma_start(S["quad_dst"][0:QUAD_ROWS, :],
                         dst_rows.rearrange("(r q) e -> r (q e)", r=QUAD_ROWS)).then_inc(s_pair, 16)
            sp.wait_ge(s_fs, 1)
            reps = TABLE // (P * FILL)
            sp.dma_start(table_e[0:TABLE, :].rearrange("(p n r) w -> p n (r w)", p=P, r=FILL),
                         E["fill"].unsqueeze(1).broadcast_to([P, reps, FILL * PAYLOAD])).then_inc(s_fill, 16)
            sp.wait_ge(s_wz, 1)
            w_list = [sage_wl, gcn_w] + [mean_wt[64 * l:64 * (l + 1), :] for l in range(3)]
            moves = []
            for l, w in enumerate(w_list):
                moves += [(w12[0:64, l, 0:64], w), (w12[64:128, l, 0:64], w), (w3[0:64, l, 0:64], w)]
            moves += [(wroot[:, :], sage_wr), (wlast[0:16, :], sage_we), (wlast[16:17, :], sage_be),
                      (wlast[17:18, :], sage_bl)]
            for k, (w, b_row) in enumerate(((wf, bf_), (ws, bs_))):
                moves += [(wpq[0:64, 64 * k:64 * (k + 1)], w[0:64, :]),
                          (wpq[0:64, 128 + 64 * k:128 + 64 * (k + 1)], w[64:128, :]),
                          (bpq[:, 128 + 64 * k:128 + 64 * (k + 1)], b_row)]
            for k, v in enumerate((gcn_b, gamma, beta)):
                moves.append((vecs[:, k, :], v.rearrange("o f -> (o f)").partition_broadcast(P)))
            for to, of in moves:
                sp.dma_start(to, of).then_inc(s_w, 16)
            n_weights = len(moves)
            e32_chunks = e32.rearrange("(c p) w -> p c w", p=P)
            for b in range(2):
                sp.dma_start(payload[:, b, :, 0:EDGE_F], e32_chunks[:, BATCH * b:BATCH * (b + 1), :]).then_inc(s_e32[b], 16)
            with sp.Fori(1, MOVED // (2 * BATCH)) as i:
                for b in range(2):
                    sp.wait_ge(s_moved[b], i * (16 * BATCH))
                    sp.dma_start(payload[:, b, :, 0:EDGE_F],
                                 e32_chunks[:, ds(i * (2 * BATCH) + BATCH * b, BATCH), :]).then_inc(s_e32[b], 16)
            sp.wait_ge(s_adj, WINDOWS + 2)
            for b in range(2):
                sp.wait_ge(s_moved[b], 16 * BATCH * (MOVED // (2 * BATCH)))
            sp.dma_start(xs, x.rearrange("(t p) f -> p t f", p=P)).then_inc(s_x, 16)
            sp.wait_ge(s_wb0, 1)
            for c in range(2):
                for k, w in enumerate((wf, ws)):
                    sp.dma_start(w_edge[PAYLOAD * c:PAYLOAD * c + EDGE_F, P * c + FEAT * k:P * c + FEAT * (k + 1)],
                                 w[2 * FEAT:2 * FEAT + EDGE_F, :]).then_inc(s_wb, 16)
            for t in range(TILES):
                sp.wait_ge(s_catU, GROUPS + t + 1)
                b = t % 2
                sp.dma_start(table_q[P * t:P * (t + 1), :], pair_of("pq", b, 128)).then_inc(s_pq[b], 16)
            groups = table_e[0:TABLE, :].rearrange("(r c) w -> r (c w)", c=4)

            def load(i, k):
                sp.wait_ge(s_tr, i * 4 + (k + 1))
                sp.wait_ge(s_now, i * 4 + (k + 1))
                sp.dma_start(pay(k), groups[ds(i * (4 * P) + P * k, P), :]).then_inc(s_pay[k], 16)

            with sp.Fori(0, SPANS // 4) as i:
                for k in range(4):
                    load(i, k)
            for k in range(SPANS % 4):
                load(SPANS // 4, k)
            sp.wait_ge(s_fin, 1)
            full = (TILES - 1) * P
            sp.dma_start(out[0:full, :].rearrange("(t p) f -> p t f", p=P), xs[:, 0:TILES - 1, :]).then_inc(s_out, 16)
            sp.dma_start(out[full:N_NODES, :], xs[0:LAST, TILES - 1, :]).then_inc(s_out, 16)
            sp.wait_ge(s_out, 32)

        @block.gpsimd
        def _(pool):
            g = nc.gpsimd
            g.iota(tmp_i[:], pattern=[[1, P]], base=0, channel_multiplier=-1)
            g.iota(B["iota"], pattern=[[1, MOV]], base=0, channel_multiplier=0)
            g.iota(S["win_i"][:, 0:WINDOWS], pattern=[[WIN, WINDOWS]], base=0, channel_multiplier=0)
            g.iota(S["win_i"][:, WINDOWS:2 * WINDOWS], pattern=[[WIN, WINDOWS]], base=WIN, channel_multiplier=0)
            g.iota(S["win_i"][:, 2 * WINDOWS:3 * WINDOWS], pattern=[[P, WINDOWS]], base=0, channel_multiplier=0)
            g.iota(pnum_i[:, 0:QPR], pattern=[[1, QPR]], base=1, channel_multiplier=QPR)
            g.iota(pnum_i[:, QPR:2 * QPR], pattern=[[-1, QPR]], base=QUADS, channel_multiplier=-QPR)
            g.iota(S["half_no"].rearrange("p (h t) -> p h t", h=2), pattern=[[1, 2], [2, TILES]], base=0,
                   channel_multiplier=0)
            g.iota(S["node_no"], pattern=[[P, TILES]], base=0, channel_multiplier=1)
            g.iota(R["dump_i"], pattern=[[1, 1]], base=TABLE, channel_multiplier=1)
            g.iota(S["edge_no"], pattern=[[1, 256]], base=1, channel_multiplier=0)
            g.iota(S["pair_no"], pattern=[[1, PAIRS]], base=1, channel_multiplier=0).then_inc(s_const, 1)
            pool.wait_ge(s_place, 1)
            pool.wait_ge(s_fill, 16)

            def move(lo, hi):
                with pool.Fori(lo, hi) as i:
                    for b in range(2):
                        batch = ds(i * (2 * BATCH) + BATCH * b, BATCH)
                        pool.wait_ge(s_e32[b], i * 16 + 16)
                        pool.sem_inc(s_go, 1)
                        g.tensor_copy(payload[:, b, :, EDGE_F:PAYLOAD], ends[:, batch, :])
                        g.tensor_copy(B["moving"][:, BATCH * b:BATCH * (b + 1)], B["edge_at"][:, batch]).then_inc(s_ids, 1)
                        pool.wait_ge(s_ids, i * 2 + (b + 1))
                        pool.sem_inc(s_go, 1)
                        for c in range(BATCH):
                            at = B["moving"][:, BATCH * b + c:BATCH * b + c + 1]
                            g.indirect_dma_start(out=table_e, out_offset=bass.IndirectOffsetOnAxis(ap=at, axis=0),
                                                 in_=payload[:, b, c, :], in_offset=None).then_inc(s_moved[b], 16)

            move(0, EARLY)
            pool.wait_ge(s_lp, 1)
            pair_rows = dst_rows.rearrange("(r a) e -> r (a e)", a=2)
            for t in range(TILES):
                g.indirect_dma_start(out=S["rows"][:, 256 * t:256 * (t + 1)], out_offset=None, in_=pair_rows,
                                     in_offset=bass.IndirectOffsetOnAxis(ap=gat_i[:, t:t + 1], axis=0)
                                     ).then_inc(s_rows, 16)
            pool.wait_ge(s_gat, 1)
            for t in range(TILES):
                g.indirect_dma_start(out=ecat[:, t, 0:EDGE_D], out_offset=None, in_=e16,
                                     in_offset=bass.IndirectOffsetOnAxis(ap=gat_e[:, t:t + 1], axis=0)
                                     ).then_inc(s_e16, 16)
            move(EARLY, MOVED // (2 * BATCH))
            pool.wait_ge(s_used, LAYERS * GROUPS + 2)
            g.iota(M["lane_i"], pattern=[[1, P]], base=0, channel_multiplier=0)
            g.iota(M["span_no"], pattern=[[1, SPANS]], base=0, channel_multiplier=0).then_inc(s_io3, 1)
            for b in range(2):
                pool.wait_ge(s_pq[b], 16 * ((TILES + 1 - b) // 2))
            pool.sem_inc(s_now, 4)

            def indices(i, k):
                pool.wait_ge(s_pay[k % 4], (i + k // 4) * 16 + 16)
                pool.sem_inc(s_go, 1)
                g.tensor_copy(M["now"][:, 4 * (k % 4):4 * (k % 4) + 4], pay_of(k % 4)[:, :, PAYLOAD - 1]).then_inc(s_now, 1)

            def gather(i, k):
                pool.wait_ge(s_now, i * 4 + (k + 5))
                pool.wait_ge(s_add, i * 4 + (k + 1))
                pool.sem_inc(s_go, 1)
                for c in range(4):
                    at = M["now"][:, 4 * (k % 4) + c:4 * (k % 4) + c + 1]
                    g.indirect_dma_start(out=pair_of("gq", k % 2, 512)[:, P * c:P * (c + 1)], out_offset=None,
                                         in_=table_q, in_offset=bass.IndirectOffsetOnAxis(ap=at, axis=0)
                                         ).then_inc(s_g[k % 2], 16)

            indices(0, 0)
            with pool.Fori(0, SPANS // 4) as i:
                for k in range(4):
                    indices(i, k + 1)
                    gather(i, k)
            indices(SPANS // 4, 1)
            gather(SPANS // 4, 0)
            gather(SPANS // 4, 1)

        @block.vector
        def _(v):
            dve = nc.vector
            chain = [0]

            def link(ins):
                chain[0] += 1
                ins.then_inc(s_ch, 1)
                v.wait_ge(s_ch, chain[0])

            dve.memset(w12[:], 0.0)
            dve.memset(bpq[:], 0.0)
            link(dve.memset(w3[:], 0.0))
            dve.memset(w3[64:65, :, 64:65], 1.0).then_inc(s_wz, 1)
            fill = E["fill"].rearrange("p (r w) -> p r w", r=FILL)
            link(dve.memset(E["fill"], 0.0))
            dve.memset(fill[:, :, EDGE_F:EDGE_F + 1], float(PAD)).then_inc(s_fs, 1)
            dve.memset(ones[:], 1.0)
            dve.memset(zeros[:], 0.0)
            v.wait_ge(s_const, 1)
            dve.tensor_scalar(ident[:], tmp_i[:], 0.0, None, ALU.is_equal)
            dve.tensor_scalar(ident16[:], tmp_i[:], 0.0, None, ALU.is_equal)
            dve.tensor_copy(wgrid[:, :, :], S["win_i"].rearrange("p (a w) -> p a w", a=3))
            link(dve.tensor_copy(pnum[:, :, :], pnum_i[:, :].rearrange("p (a t) -> p a t", a=2)))
            v.wait_ge(s_pair, 16)
            r = slice(0, QUAD_ROWS)
            pd = S["quad_dst"][r, :].rearrange("p (q e) -> p q e", q=QPR)
            dve.tensor_reduce(bounds[r, 0:QPR], pd, AX.X, ALU.min)
            link(dve.tensor_reduce(bounds[r, QPR:2 * QPR], pd, AX.X, ALU.max))
            for q in range(QPR):
                dve.tensor_scalar(hit[r, q, 0, :], wgrid[r, 0, :], bounds[r, QPR + q:QPR + q + 1], None, ALU.is_le).then_inc(s_ch, 1)
            chain[0] += QPR
            v.wait_ge(s_ch, chain[0])
            for q in range(QPR):
                dve.scalar_tensor_tensor(hit[r, q, 0, :], wgrid[r, 1, :], bounds[r, q:q + 1], hit[r, q, 0, :],
                                         ALU.is_gt, ALU.mult).then_inc(s_ch, 1)
            chain[0] += QPR
            v.wait_ge(s_ch, chain[0])
            for q in range(QPR):
                dve.tensor_scalar(hit[r, q, 1, :], hit[r, q, 0, :], pnum[r, 0, q:q + 1], None, ALU.mult).then_inc(s_ch, 1)
            chain[0] += QPR
            v.wait_ge(s_ch, chain[0])
            for q in range(QPR):
                last = dve.tensor_scalar(hit[r, q, 0, :], hit[r, q, 0, :], pnum[r, 1, q:q + 1], None, ALU.mult)
            last.then_inc(s_hit, 1)
            v.wait_ge(s_in, 32)
            src_i, dst_i, ka, kb = S["src_i"], S["dst_i"], S["ka"], S["kb"]
            dve.tensor_scalar(ka, dst_i, 6, 7, ALU.logical_shift_right, ALU.logical_shift_left)
            link(dve.tensor_scalar(kb, src_i, P - 1, None, ALU.bitwise_and))
            link(dve.tensor_tensor(B["key_lo"], ka, kb, ALU.add))
            dve.tensor_scalar(ka, src_i, 7, 6, ALU.logical_shift_right, ALU.logical_shift_left)
            link(dve.tensor_scalar(kb, dst_i, WIN - 1, None, ALU.bitwise_and))
            link(dve.tensor_tensor(B["key_mv"], ka, kb, ALU.add))
            dve.tensor_scalar(S["dhi"], dst_i, 6, None, ALU.logical_shift_right)
            dve.tensor_copy(S["dlo"], kb).then_inc(s_ch, 1)
            chain[0] += 1
            v.wait_ge(s_ch, chain[0])
            v.wait_ge(s_hitT, 1)
            dve.tensor_reduce(ext[:, 0:1], ps[0:WINDOWS, 0:QUADS], AX.X, ALU.max)
            dve.tensor_reduce(ext[:, 1:2], ps[0:WINDOWS, 512:512 + QUADS], AX.X, ALU.max).then_inc(s_ext, 1)
            v.wait_ge(s_extT, 1)
            er = ps[0:1, 1024:1024 + 2 * WINDOWS]
            link(dve.memset(row[:, 4, :], 0.0))
            link(dve.tensor_scalar(row[:, 0, :], er[:, 0:WINDOWS], -1.0, float(QUADS), ALU.mult, ALU.add))
            link(dve.tensor_scalar(row[:, 0, :], row[:, 0, :], float(QUADS - 3), None, ALU.min))
            link(dve.tensor_tensor(row[:, 1, :], er[:, WINDOWS:2 * WINDOWS], row[:, 0, :], ALU.subtract))
            link(dve.tensor_scalar(row[:, 1, :], row[:, 1, :], 3.0, None, ALU.max))
            link(dve.tensor_tensor_scan(row[:, 2, :], row[:, 1, :], row[:, 4, :], 0.0, ALU.add, ALU.add))
            link(dve.tensor_tensor(row[:, 3, :], row[:, 2, :], row[:, 1, :], ALU.subtract))
            dve.tensor_copy(trip[:, 0:2, :], row[:, 0:2, :])
            link(dve.tensor_copy(trip[:, 2, :], row[:, 3, :]))
            link(dve.tensor_scalar(E["before"], tmp_i[:], 0.0, None, ALU.is_gt))
            link(dve.tensor_scalar(kb, src_i, 7, None, ALU.logical_shift_right))
            dve.tensor_copy(R["dump"], R["dump_i"])
            link(dve.tensor_copy(R["tile_f"], kb))
            for t in range(TILES):
                dve.tensor_scalar(oh_tile[:, t, :], R["tile_f"], float(t), None, ALU.is_equal).then_inc(s_tiles, 1)
            link(dve.tensor_scalar(kb, src_i, P - 1, None, ALU.bitwise_and))
            dve.tensor_copy(ends[:, :, 0], kb)
            dve.tensor_copy(ends[:, :, 1], dst_i)
            v.wait_ge(s_pre, 1)
            total, earlier = bank(3)[:, 0:TILES], bank(3)[:, 64:64 + TILES]
            link(dve.tensor_scalar(R["spans"], total, float(SPAN - 1), None, ALU.add))
            link(dve.tensor_copy(R["spans_i"], R["spans"]))
            link(dve.tensor_scalar(R["spans_i"], R["spans_i"], 9, None, ALU.logical_shift_right))
            link(dve.tensor_copy(R["spans"], R["spans_i"]))
            link(dve.tensor_scalar(R["spans"], R["spans"], 1.0, None, ALU.max))
            link(dve.tensor_tensor_scan(R["upto"], R["spans"], ones[:, 0:TILES], 0.0, ALU.add, ALU.mult))
            link(dve.tensor_tensor(span0[:], R["upto"], R["spans"], ALU.subtract))
            link(dve.tensor_scalar(R["base"], span0[:], float(SPAN), -1.0, ALU.mult, ALU.add))
            link(dve.tensor_tensor(R["base"], R["base"], earlier, ALU.add))
            link(dve.memset(R["at"], 0.0))
            end = slice(MOVED - 1, MOVED)
            link(dve.tensor_scalar(R["at"][:, end], R["tile_f"][:, end], float(PAD >> 7), R["dump"], ALU.is_equal, ALU.mult))
            rank, mine, at = R["rank"], R["mine"], R["at"]
            every = ones[:, 0:1].broadcast_to([P, CHUNKS])
            with v.Fori(0, TILES) as t:
                own = oh_tile[:, ds(t, 1), :].rearrange("p o c -> p (o c)")
                dve.tensor_tensor_scan(rank, own, every, R["base"][:, ds(t, 1)], ALU.add, ALU.mult).then_inc(s_rank, 1)
                v.wait_ge(s_rank, t * 3 + 1)
                dve.tensor_tensor(mine, rank, own, ALU.mult).then_inc(s_rank, 1)
                v.wait_ge(s_rank, t * 3 + 2)
                dve.tensor_tensor(at, at, mine, ALU.add).then_inc(s_rank, 1)
                v.wait_ge(s_rank, t * 3 + 3)
            dve.tensor_copy(B["edge_at"], at).then_inc(s_place, 1)
            v.wait_ge(s_place, 1)
            dlo2, dhi2 = (S[k].rearrange("p (b c n) -> p b c n", b=2, c=BLOCK) for k in ("oh_dlo", "oh_dhi"))

            def destination_rows(u, b):
                v.wait_ge(s_seen_c, u + 1)
                chunks = ds(u * BLOCK, BLOCK)
                for to, number, key, n in ((dlo2, B["iota"], S["dlo"], WIN), (dhi2, S["half_no"], S["dhi"], WINDOWS)):
                    big = [P, BLOCK, n]
                    last = dve.tensor_tensor(to[:, b, :, :], number[:, 0:n].unsqueeze(1).broadcast_to(big),
                                             key[:, chunks].unsqueeze(2).broadcast_to(big), ALU.is_equal)
                last.then_inc(s_seen_o, 1)

            v.sem_inc(s_seen_c, 2)
            with v.Fori(0, CHUNKS // (2 * BLOCK)) as i:
                for b in range(2):
                    destination_rows(i * 2 + b, b)
            destination_rows(CHUNKS // BLOCK - 1, 0)
            v.wait_ge(s_seen_a, CHUNKS // BLOCK + 2)
            big = [P, PAIRS, TILES]
            link(dve.scalar_tensor_tensor(
                S["seen_at"].rearrange("p (r t) -> p r t", t=TILES), S["seen"].rearrange("p (r t) -> p r t", t=TILES),
                0.0, S["pair_no"].unsqueeze(2).broadcast_to(big), ALU.is_gt, ALU.mult))
            link(dve.tensor_reduce(last_pair[:], S["seen_at"].rearrange("p (r t) -> p t r", t=TILES), AX.X, ALU.max))
            dve.tensor_scalar(gat_i[:], last_pair[:], -1.0, 0.0, ALU.add, ALU.max).then_inc(s_lp, 1)
            v.wait_ge(s_rows, 16 * TILES)
            rows = S["rows"].rearrange("p (t e) -> p t e", t=TILES)
            big = [P, TILES, 256]
            link(dve.tensor_tensor(rows, rows, S["node_no"].unsqueeze(2).broadcast_to(big), ALU.is_equal))
            link(dve.tensor_tensor(rows, rows, S["edge_no"].unsqueeze(1).broadcast_to(big), ALU.mult))
            link(dve.tensor_reduce(stat[:, 0, :], rows, AX.X, ALU.max))
            link(dve.tensor_scalar(stat[:, 1, :], last_pair[:], 256.0, -257.0, ALU.mult, ALU.add))
            link(dve.tensor_tensor(stat[:, 1, :], stat[:, 1, :], stat[:, 0, :], ALU.add))
            link(dve.tensor_scalar(stat[:, 1, :], stat[:, 1, :], 0.0, None, ALU.max))
            dve.tensor_copy(gat_e[:], stat[:, 1, :]).then_inc(s_gat, 1)
            link(dve.tensor_copy(B["iota_f"], B["iota"][:, 0:P]))
            v.wait_ge(s_gat, 1)
            v.wait_ge(s_fill, 16)
            v.sem_inc(s_ready, 1)

            def window_chunks(w, first, before, j):
                for a in range(4):
                    v.wait_ge(s_chunk, (before + j) * 4 + (a + 1))
                    dve.tensor_scalar(oh_mv[:, a, :], B["iota"], B["key_mv"][:, chunk_of(first, j, a)], None,
                                      ALU.is_equal).then_inc(s_oh, 1)

            with v.Fori(0, WINDOWS // RUN) as i:
                trip_now = window_trip(v, i * RUN)
                for s in range(RUN):
                    w, trip_next = i * RUN + s, []
                    first, count, before = trip_now
                    for j in range(2):
                        window_chunks(w, first, before, j)
                        if s + 1 < RUN:
                            trip_next.append(trip_value(v, w + 1, j))
                    with v.Fori(2, count) as j:
                        window_chunks(w, first, before, j)
                    if s + 1 < RUN:
                        trip_now = trip_next + [trip_value(v, w + 1, 2)]

            v.wait_ge(s_adj, WINDOWS + 2)
            v.wait_ge(s_w, 16 * n_weights)
            link(dve.tensor_scalar(stat[:, 1, :], last_pair[:], 0.0, None, ALU.is_gt))
            dve.memset(ecat[:, :, EDGE_D + 1:ECAT], 1.0)
            link(dve.tensor_copy(ecat[:, :, EDGE_D], stat[:, 1, :]))
            v.wait_ge(s_x, 16)

            wide = [P, TILES, FEAT]

            def over(s):
                return s.unsqueeze(2).broadcast_to(wide)

            n_std = [0]

            def layernorm_relu():
                link(dve.tensor_reduce(stat[:, 0, :], xs, AX.X, ALU.add))
                link(dve.tensor_scalar(stat[:, 0, :], stat[:, 0, :], -1.0 / FEAT, None, ALU.mult))
                link(dve.tensor_tensor(hs, xs, over(stat[:, 0, :]), ALU.add))
                link(dve.tensor_tensor(ts, hs, hs, ALU.mult))
                link(dve.tensor_reduce(stat[:, 1, :], ts, AX.X, ALU.add))
                dve.tensor_scalar(stat[:, 1, :], stat[:, 1, :], 1.0 / FEAT, 1e-5, ALU.mult, ALU.add).then_inc(s_var, 1)
                n_std[0] += 1
                v.wait_ge(s_std, n_std[0])
                link(dve.reciprocal(stat[:, 2, :], stat[:, 2, :]))
                link(dve.tensor_tensor(hs, hs, over(stat[:, 2, :]), ALU.mult))
                link(dve.tensor_scalar(hs, hs, 0.0, None, ALU.max))

            def split_y(y, l):
                link(dve.tensor_copy(y12[:, :, 0:FEAT], y))
                link(dve.tensor_tensor(ts, y, y12[:, :, 0:FEAT], ALU.subtract))
                link(dve.tensor_copy(y12[:, :, FEAT:2 * FEAT], ts))
                dve.tensor_tensor(y3[:, :, 0:FEAT], ts, y12[:, :, FEAT:2 * FEAT], ALU.subtract).then_inc(s_y, 1)

            link(dve.memset(y3[:, :, FEAT:FEAT + 2], 1.0))
            ps3 = [bank(2), bank(3)]
            po = [bank(4), bank(5)]
            for l in range(LAYERS):
                if l in (0, 1, 2):
                    layernorm_relu()
                if l == 0:
                    split_y(hs, l)
                elif l == 1:
                    link(dve.tensor_tensor(ts, hs, over(scale[:, 1, :]), ALU.mult))
                    split_y(ts, l)
                elif l == 2:
                    split_y(hs, l)
                else:
                    split_y(ts, l)
                for g in range(GROUPS):
                    b, n = g % 2, min(4, TILES - 4 * g)
                    G = GROUPS * l + g
                    v.wait_ge(s_agg, G + 1)
                    if G >= 2:
                        v.wait_ge(s_proj, G - 1)
                    dve.tensor_copy(t3[0:65, b, 0:P * n], ps3[b][0:65, 0:P * n]).then_inc(s_t3, 1)
                    v.wait_ge(s_proj, G + 1)
                    o = po[b].rearrange("p (t w) -> p t w", w=P)
                    tt = slice(4 * g, 4 * g + n)
                    sc = scale[:, min(l, 2), tt]
                    if l == 0:
                        link(dve.tensor_copy(cnt[:, tt], o[:, 0:n, 64]))
                        link(dve.tensor_scalar(scale[:, 0, tt], cnt[:, tt], 1.0, None, ALU.max))
                        link(dve.reciprocal(scale[:, 0, tt], scale[:, 0, tt]))
                    dve.tensor_tensor(ts[:, tt, :], o[:, 0:n, 0:FEAT], sc.unsqueeze(2).broadcast_to([P, n, FEAT]),
                                      ALU.mult).then_inc(s_used, 1)
                v.wait_ge(s_used, GROUPS * (l + 1) + 2)
                if l == 0:
                    v.wait_ge(s_e16, 16 * TILES)
                    dve.tensor_tensor(ecat[:, :, 0:EDGE_D], ecat[:, :, 0:EDGE_D],
                                      ecat[:, :, EDGE_D:EDGE_D + 1].broadcast_to([P, TILES, EDGE_D]),
                                      ALU.mult).then_inc(s_cat, 1)
                    d24 = adj[:, 0:(TILES - 1) * (NPAD + P)].rearrange("p (k d) -> p k d", k=TILES - 1)[:, :, 0:P]
                    link(dve.tensor_tensor(d24, d24, ident16[:, :].unsqueeze(1).broadcast_to([P, TILES - 1, P]), ALU.add))
                    dl = A3[:, TILES - 1, NPAD - P:NPAD]
                    link(dve.tensor_tensor(dl, dl, ident16[:, :], ALU.add))
                    link(dve.tensor_scalar(scale[:, 2, :], cnt[:, :], 1.0, None, ALU.add))
                    link(dve.reciprocal(scale[:, 2, :], scale[:, 2, :]))
                    dve.tensor_copy(stat[:, 1, :], scale[:, 2, :]).then_inc(s_var, 1)
                    n_std[0] += 1
                    v.wait_ge(s_std, n_std[0])
                    link(dve.tensor_copy(scale[:, 1, :], stat[:, 2, :]))
                    link(dve.tensor_tensor(xs, xs, ts, ALU.add))
                    for g in range(GROUPS):
                        n = min(4, TILES - 4 * g)
                        v.wait_ge(s_catO, g + 1)
                        dve.tensor_tensor(xs[:, 4 * g:4 * g + n, :], xs[:, 4 * g:4 * g + n, :],
                                          bank(0, FEAT * n).rearrange("p (t f) -> p t f", f=FEAT),
                                          ALU.add).then_inc(s_catU, 1)
                    v.wait_ge(s_catU, GROUPS)
                elif l == 1:
                    link(dve.tensor_tensor(xs, xs, ts, ALU.add))
                    link(dve.tensor_tensor(xs, xs, vecs[:, 0:1, :].broadcast_to(wide), ALU.add))
                elif l == 4:
                    link(dve.tensor_tensor(xs, xs, ts, ALU.add))
            layernorm_relu()
            v.sem_inc(s_cat, 1)
            dve.memset(w_edge, 0.0).then_inc(s_wb0, 1)
            pf = M["pf"].rearrange("p (t w) -> p t w", t=TILES)
            p3 = M["p3"].rearrange("p (t k w) -> p t k w", t=TILES, k=3)
            for t in range(TILES):
                b = t % 2
                v.wait_ge(s_catO, GROUPS + t + 1)
                if t >= 2:
                    v.wait_ge(s_pq[b], 16 * (t // 2))
                dve.tensor_copy(pf[:, t, :], bank(b, 128))
                dve.tensor_copy(pair_of("pq", b, 128), bank(b, 256)[:, 128:256]).then_inc(s_catU, 1)
            v.wait_ge(s_catU, GROUPS + TILES)
            link(dve.memset(M["zeros"], 0.0))
            link(dve.tensor_copy(p3[:, :, 0, :], pf))
            link(dve.tensor_tensor(pf, pf, p3[:, :, 0, :], ALU.subtract))
            link(dve.tensor_copy(p3[:, :, 1, :], pf))
            link(dve.tensor_tensor(p3[:, :, 2, :], pf, p3[:, :, 1, :], ALU.subtract))
            v.wait_ge(s_io3, 1)
            upto = M["is_upto"][0:1, :].rearrange("p (s t) -> p s t", t=TILES)
            big = [1, SPANS, TILES]
            link(dve.tensor_tensor(upto, M["span_no"][0:1, :].unsqueeze(2).broadcast_to(big),
                                   span0[0:1, :].unsqueeze(1).broadcast_to(big), ALU.is_ge))
            link(dve.tensor_reduce(M["tile_f"][0:1, :], upto, AX.X, ALU.add))
            link(dve.tensor_scalar(M["tile_f"][0:1, :], M["tile_f"][0:1, :], -1.0, None, ALU.add))
            link(dve.tensor_copy(M["tile_of"][0:1, :], M["tile_f"][0:1, :]))
            dve.tensor_copy(M["lane"], M["lane_i"]).then_inc(s_p3, 1)
            v.wait_ge(s_p3, 1)
            v.sem_inc(s_add, 2)
            def source_rows(i, k):
                v.wait_ge(s_pay[k % 4], (i + k // 4) * 16 + 16)
                v.wait_ge(s_sc, i * 4 + (k + 1))
                big = [P, 4, P]
                dve.tensor_tensor(M["oh"][:, 512 * (k % 4):512 * (k % 4) + 512].rearrange("p (c n) -> p c n", c=4),
                                  M["lane"].unsqueeze(1).broadcast_to(big),
                                  pay_of(k % 4)[:, :, EDGE_F:EDGE_F + 1].broadcast_to(big),
                                  ALU.is_equal).then_inc(s_oh3, 1)

            def add_rows(i, k):
                b = k % 2
                v.wait_ge(s_z, i * 4 + (k + 1))
                v.wait_ge(s_g[b], (i * 2 + k // 2) * 64 + 64)
                dve.tensor_tensor(pair_of("z", b, 512), bank(4 + 3 * b), pair_of("gq", b, 512),
                                  ALU.add).then_inc(s_add, 1)

            def by_chunk(name, b, n):
                return pair_of(name, b, 4 * n).rearrange("p (c w) -> p c w", w=n)

            def softplus(i, k):
                b = k % 2
                z3, ln3 = by_chunk("z", b, P), by_chunk("ln", b, P)
                v.wait_ge(s_ln, i * 4 + (k + 1))
                dve.scalar_tensor_tensor(by_chunk("val", b, FEAT), z3[:, :, FEAT:P], 0.0, ln3[:, :, FEAT:P],
                                         ALU.max, ALU.add)
                dve.scalar_tensor_tensor(by_chunk("gate", b, FEAT), z3[:, :, 0:FEAT], 0.0, ln3[:, :, 0:FEAT],
                                         ALU.min, ALU.subtract).then_inc(s_ga, 1)

            def message(i, k):
                b = k % 2
                hm, m1, m2, m3 = M["hm"], *(pair_of(m, b, 256) for m in ("m1", "m2", "m3"))
                v.wait_ge(s_gt, i * 4 + (k + 1))
                dve.tensor_tensor(hm, pair_of("gate", b, 256), pair_of("val", b, 256), ALU.mult).then_inc(s_hm, 1)
                v.wait_ge(s_sc, i * 4 + (k + 3))
                v.wait_ge(s_hm, i * 4 + (k + 1))
                dve.tensor_copy(m1, hm).then_inc(s_m1, 1)
                v.wait_ge(s_m1, i * 4 + (k + 1))
                dve.tensor_tensor(hm, hm, m1, ALU.subtract).then_inc(s_r1, 1)
                v.wait_ge(s_r1, i * 4 + (k + 1))
                dve.tensor_copy(m2, hm).then_inc(s_m2, 1)
                v.wait_ge(s_m2, i * 4 + (k + 1))
                dve.tensor_tensor(m3, hm, m2, ALU.subtract).then_inc(s_m3, 1)

            source_rows(0, 0)
            source_rows(0, 1)
            add_rows(0, 0)
            with v.Fori(0, SPANS // 4) as i:
                for k in range(4):
                    source_rows(i, k + 2)
                    softplus(i, k)
                    add_rows(i, k + 1)
                    message(i, k)
            softplus(SPANS // 4, 0)
            add_rows(SPANS // 4, 1)
            message(SPANS // 4, 0)
            softplus(SPANS // 4, 1)
            message(SPANS // 4, 1)
            link(dve.tensor_tensor(xs, xs, hs, ALU.add))
            v.wait_ge(s_tile, 1)
            msg = M["msg"].rearrange("p (t f) -> p t f", f=FEAT)
            dve.tensor_copy(M["msg"], ps[:, 0:TILES * FEAT]).then_inc(s_msg, 1)
            v.wait_ge(s_sum, 1)
            link(dve.tensor_scalar(bn[:, 0, :], bank(6, FEAT), -1.0 / N_NODES, None, ALU.mult))
            link(dve.tensor_tensor(msg, msg, bn[:, 0:1, :].broadcast_to(wide), ALU.add))
            dve.tensor_tensor(ts, msg, msg, ALU.mult).then_inc(s_sq, 1)
            v.wait_ge(s_sqs, 1)
            dve.tensor_scalar(bn[:, 1, :], bank(7, FEAT), 1.0 / N_NODES, 1e-5, ALU.mult, ALU.add).then_inc(s_bnv, 1)
            v.wait_ge(s_bns, 1)
            link(dve.reciprocal(bn[:, 2, :], bn[:, 2, :]))
            link(dve.tensor_tensor(bn[:, 2, :], bn[:, 2, :], vecs[:, 1, :], ALU.mult))
            link(dve.tensor_tensor(msg, msg, bn[:, 2:3, :].broadcast_to(wide), ALU.mult))
            link(dve.tensor_tensor(msg, msg, vecs[:, 2:3, :].broadcast_to(wide), ALU.add))
            dve.tensor_tensor(xs, xs, msg, ALU.add).then_inc(s_fin, 1)

        @block.scalar
        def _(act):
            a = nc.scalar
            a.preload_act_table(ACT.Sqrt)
            for t in range(TILES):
                act.wait_ge(s_tiles, t + 1)
                last = a.activation(oh_tile[:, t, :], oh_tile[:, t, :], ACT.Identity,
                                    accum_out=R["counts"][:, t:t + 1])
            last.then_inc(s_counts, 1)
            act.sem_inc(s_seen_a, 2)

            def keep_counts(u, b):
                act.wait_ge(s_seen_c, u + 3)
                n = BLOCK // 2 * TILES
                a.copy(S["seen"][:, ds(u * n, n)], bank(4 + b, n)).then_inc(s_seen_a, 1)

            with act.Fori(0, CHUNKS // (2 * BLOCK)) as i:
                for b in range(2):
                    keep_counts(i * 2 + b, b)
            keep_counts(CHUNKS // BLOCK - 1, 0)
            act.wait_ge(s_ready, 1)
            act.sem_inc(s_adj, 2)

            def low_rows(base, first, before, j):
                for h in range(2):
                    act.wait_ge(s_chunk, (before + j) * 4 + (2 * h + 2))
                    for c in range(2 * h, 2 * h + 2):
                        last = a.activation(lo_far[:, c, :], base, ACT.Abs, scale=-1.0,
                                            bias=B["key_lo"][:, chunk_of(first, j, c)])
                    last.then_inc(s_far, 1)
                    act.wait_ge(s_far, (before + j) * 2 + (h + 1))
                    a.activation(oh_lo[:, 2 * h:2 * h + 2, :], lo_far[:, 2 * h:2 * h + 2, :], ACT.Relu,
                                 scale=-1.0, bias=1.0).then_inc(s_lo, 1)

            def window_copy(b, w):
                act.wait_ge(s_win, w + 1)
                a.copy(A3[:, :, ds(w * WIN, WIN)],
                       adj_acc[b].rearrange("p (k d) -> p k d", d=WIN)).then_inc(s_adj, 1)

            lo_base = [B["lo_base"][:, P * b:P * (b + 1)] for b in range(2)]

            def window_base(b, w):
                a.activation(lo_base[b], B["iota_f"], ACT.Identity, bias=wgrid[:, 2, ds(w, 1)]).then_inc(s_base, 1)

            with act.Fori(0, WINDOWS // RUN) as i:
                trip_now = window_trip(act, i * RUN)
                window_base(0, i * RUN)
                for s in range(RUN):
                    b, w, trip_next = s % 2, i * RUN + s, []
                    first, count, before = trip_now
                    act.wait_ge(s_base, w + 1)
                    low_rows(lo_base[b], first, before, 0)
                    if s:
                        window_copy(1 - b, w - 1)
                    if s + 1 < RUN:
                        window_base(1 - b, w + 1)
                        trip_next.append(trip_value(act, w + 1, 0))
                    low_rows(lo_base[b], first, before, 1)
                    if s + 1 < RUN:
                        trip_next.append(trip_value(act, w + 1, 1))
                    with act.Fori(2, count) as j:
                        low_rows(lo_base[b], first, before, j)
                    if s + 1 < RUN:
                        trip_now = trip_next + [trip_value(act, w + 1, 2)]
                window_copy(1, i * RUN + RUN - 1)
            n_var = [0]

            def root():
                n_var[0] += 1
                act.wait_ge(s_var, n_var[0])
                a.activation(stat[:, 2, :], stat[:, 1, :], ACT.Sqrt).then_inc(s_std, 1)

            def cat_group(at, with_last):
                g = at % GROUPS
                b, n = g % 2, min(4, TILES - 4 * g)
                act.wait_ge(s_catT, at + 1)
                if with_last:
                    a.copy(t3[0:ECAT, b, 0:P * n], bank(7)[0:ECAT, 0:P * n])
                a.copy(t12[0:FEAT, b, 0:P * n], bank(6)[0:FEAT, 0:P * n]).then_inc(s_catS, 1)

            for l in range(LAYERS):
                if l < 3:
                    root()
                for g in range(GROUPS):
                    b, n = g % 2, min(4, TILES - 4 * g)
                    G = GROUPS * l + g
                    act.wait_ge(s_agg, G + 1)
                    if G >= 2:
                        act.wait_ge(s_proj, G - 1)
                    a.copy(t12[:, b, 0:P * n], bank(b, P * n)).then_inc(s_t12, 1)
                if l == 0:
                    root()
                    for g in range(GROUPS):
                        cat_group(g, True)
            root()
            for g in range(GROUPS):
                cat_group(GROUPS + g, False)
            a.preload_act_table_set("natural_log_exp_and_others")
            def turned(i, k):
                b = k % 2
                act.wait_ge(s_tr, i * 4 + (k + 5))
                if k >= 2:
                    act.wait_ge(s_z, i * 4 + (k - 1))
                a.copy(pair_of("oht", b, 512), bank(5))
                a.copy(pair_of("et", b, 2 * P)[0:2 * PAYLOAD, :], bank(6, 2 * P)[0:2 * PAYLOAD, :]).then_inc(s_ct, 1)

            def logs(i, k):
                b = k % 2
                z, ab = pair_of("z", b, 512), pair_of("ab", b, 512)
                act.wait_ge(s_add, i * 4 + (k + 3))
                a.activation(ab, z, ACT.Abs).then_inc(s_ab, 1)
                act.wait_ge(s_ab, i * 4 + (k + 1))
                a.activation(ab, ab, ACT.Exp, scale=-1.0).then_inc(s_ex, 1)
                act.wait_ge(s_ex, i * 4 + (k + 1))
                a.activation(pair_of("ln", b, 512), ab, ACT.Ln, bias=1.0).then_inc(s_ln, 1)

            def gate(i, k):
                g = pair_of("gate", k % 2, 256)
                act.wait_ge(s_ga, i * 4 + (k + 1))
                a.activation(g, g, ACT.Exp).then_inc(s_gt, 1)

            turned(0, 0)
            turned(0, 1)
            logs(0, 0)
            with act.Fori(0, SPANS // 4) as i:
                for k in range(4):
                    gate(i, k)
                    turned(i, k + 2)
                    logs(i, k + 1)
            gate(SPANS // 4, 0)
            logs(SPANS // 4, 1)
            gate(SPANS // 4, 1)
            act.wait_ge(s_bnv, 1)
            a.activation(bn[:, 2, :], bn[:, 1, :], ACT.Sqrt).then_inc(s_bns, 1)

        @block.tensor
        def _(pe):
            mm = nc.tensor.matmul
            pe.wait_ge(s_hit, 1)
            r = slice(0, QUAD_ROWS)
            for a in range(2):
                for q in range(QPR):
                    last = mm(ps[0:WINDOWS, 512 * a + q * QUAD_ROWS:512 * a + (q + 1) * QUAD_ROWS],
                              hit[r, q, a, :], ident[r, 0:QUAD_ROWS], start=True, stop=True)
            last.then_inc(s_hitT, 1)
            pe.wait_ge(s_ext, 1)
            for a in range(2):
                last = mm(ps[0:1, 1024 + WINDOWS * a:1024 + WINDOWS * (a + 1)], ext[:, a:a + 1],
                          ident[0:WINDOWS, 0:WINDOWS], start=True, stop=True)
            last.then_inc(s_extT, 1)
            pe.wait_ge(s_counts, 1)
            mm(bank(3)[:, 0:TILES], ones[:, :], R["counts"], start=True, stop=True)
            mm(bank(3)[:, 64:64 + TILES], E["before"], R["counts"], start=True, stop=True).then_inc(s_pre, 1)
            dlo2, dhi2 = (S[k].rearrange("p (b c n) -> p b c n", b=2, c=BLOCK) for k in ("oh_dlo", "oh_dhi"))

            def count_block(u, b):
                pe.wait_ge(s_seen_a, u + 1)
                pe.wait_ge(s_seen_o, u + 1)
                for r in range(BLOCK // 2):
                    for h in range(2):
                        o = bank(4 + b)[WIN * h:WIN * (h + 1), TILES * r:TILES * (r + 1)]
                        for c in range(2):
                            last = mm(o, dlo2[:, b, 2 * r + c, :], dhi2[:, b, 2 * r + c, TILES * h:TILES * (h + 1)],
                                      start=(c == 0), stop=(c == 1))
                last.then_inc(s_seen_c, 1)

            with pe.Fori(0, CHUNKS // (2 * BLOCK)) as i:
                for b in range(2):
                    count_block(i * 2 + b, b)
            count_block(CHUNKS // BLOCK - 1, 0)
            pe.wait_ge(s_ready, 1)
            pe.sem_inc(s_chunk, 4)

            def window_chunks(b, first, before, j, start):
                for a in range(4):
                    if a % 2 == 0:
                        pe.wait_ge(s_lo, (before + j) * 2 + (a // 2 + 1))
                    pe.wait_ge(s_oh, (before + j) * 4 + (a + 1))
                    for lo in range(0, MOV, 512):
                        n = min(512, MOV - lo)
                        last = mm(adj_acc[b][:, lo:lo + n], oh_lo[:, a, :], oh_mv[:, a, lo:lo + n],
                                  start=start and a == 0, stop=False)
                    last.then_inc(s_chunk, 1)

            with pe.Fori(0, WINDOWS // RUN) as i:
                trip_now = window_trip(pe, i * RUN)
                for s in range(RUN):
                    b, w, trip_next = s % 2, i * RUN + s, []
                    first, count, before = trip_now
                    pe.wait_ge(s_adj, w + 1)
                    for j in range(2):
                        window_chunks(b, first, before, j, j == 0)
                        if s + 1 < RUN:
                            trip_next.append(trip_value(pe, w + 1, j))
                    with pe.Fori(2, count) as j:
                        window_chunks(b, first, before, j, False)
                    for lo in range(0, MOV, 512):
                        last = mm(adj_acc[b][:, lo:lo + 1], zeros[:, :], zeros[:, 0:1], start=False, stop=True)
                    last.then_inc(s_win, 1)
                    if s + 1 < RUN:
                        trip_now = trip_next + [trip_value(pe, w + 1, 2)]

            def aggregate(l, g):
                b, n = g % 2, min(4, TILES - 4 * g) * P
                G = GROUPS * l + g
                if G >= 2:
                    pe.wait_ge(s_t12, G - 1)
                    pe.wait_ge(s_t3, G - 1)
                for k in range(TILES):
                    mm(bank(b, n), y12[:, k, :], A3[:, k, 512 * g:512 * g + n], start=(k == 0), stop=(k == TILES - 1))
                for k in range(TILES):
                    last = mm(bank(2 + b)[0:65, 0:n], y3[:, k, 0:65], A3[:, k, 512 * g:512 * g + n],
                              start=(k == 0), stop=(k == TILES - 1))
                last.then_inc(s_agg, 1)

            def project(l, g):
                b = g % 2
                G = GROUPS * l + g
                pe.wait_ge(s_t12, G + 1)
                pe.wait_ge(s_t3, G + 1)
                pe.wait_ge(s_used, G + 1)
                for i in range(min(4, TILES - 4 * g)):
                    o = ps[:, 512 * (4 + b) + P * i:512 * (4 + b) + P * i + 65]
                    mm(o, t12[:, b, P * i:P * (i + 1)], w12[:, l, :], start=True, stop=False)
                    last = mm(o, t3[0:65, b, P * i:P * (i + 1)], w3[:, l, :], start=False, stop=True)
                last.then_inc(s_proj, 1)

            def cat_group(at, with_last):
                g = at % GROUPS
                n = min(4, TILES - 4 * g)
                for i in range(n):
                    last = nc.tensor.transpose(bank(6)[0:FEAT, P * i:P * (i + 1)], hs[:, 4 * g + i, :], ident[:, :])
                    if with_last:
                        last = nc.tensor.transpose(bank(7)[0:ECAT, P * i:P * (i + 1)], ecat[:, 4 * g + i, :], ident[:, :])
                last.then_inc(s_catT, 1)
                pe.wait_ge(s_catS, at + 1)

            pe.wait_ge(s_w, 16 * n_weights)
            pe.sem_inc(s_used, 2)
            for l in range(LAYERS):
                pe.wait_ge(s_y, l + 1)
                if l == 1:
                    pe.wait_ge(s_catU, GROUPS)
                for g in range(GROUPS):
                    aggregate(l, g)
                    if g:
                        project(l, g - 1)
                project(l, GROUPS - 1)
                if l == 0:
                    pe.wait_ge(s_cat, 1)
                    for g in range(GROUPS):
                        b, n = g % 2, min(4, TILES - 4 * g)
                        cat_group(g, True)
                        if g:
                            pe.wait_ge(s_catU, g)
                        for i in range(n):
                            o = bank(0)[:, FEAT * i:FEAT * (i + 1)]
                            mm(o, t12[0:FEAT, b, P * i:P * (i + 1)], wroot[:, :], start=True, stop=False)
                            last = mm(o, t3[0:ECAT, b, P * i:P * (i + 1)], wlast[:, :], start=False, stop=True)
                        last.then_inc(s_catO, 1)
            pe.wait_ge(s_cat, 2)
            for g in range(GROUPS):
                b, n = g % 2, min(4, TILES - 4 * g)
                cat_group(GROUPS + g, False)
                for i in range(n):
                    t = 4 * g + i
                    if t >= 2:
                        pe.wait_ge(s_catU, GROUPS + t - 1)
                    o = bank(t % 2, 4 * FEAT)
                    mm(o, t12[0:FEAT, b, P * i:P * (i + 1)], wpq[:, :], start=True, stop=False)
                    mm(o, ones[0:1, :], bpq[:, :], start=False, stop=True).then_inc(s_catO, 1)
            pe.wait_ge(s_p3, 1)
            pe.wait_ge(s_wb, 16 * 4)
            for k in range(4):
                mm(bank(k), M["zeros"][:, 0:P], M["zeros"][:, 0:512], start=True, stop=False)
            pe.sem_inc(s_tr, 4)
            pe.sem_inc(s_sc, 4)

            def turn(i, k):
                slot = k % 4
                pe.wait_ge(s_oh3, i * 4 + (k + 1))
                if k >= 1:
                    pe.wait_ge(s_ct, i * 4 + k)
                for c in range(4):
                    mm(bank(5)[:, P * c:P * (c + 1)], M["oh"][:, 512 * slot + P * c:512 * slot + P * (c + 1)],
                       ident16[:, :], start=True, stop=True)
                for h in range(2):
                    last = nc.tensor.transpose(bank(6)[0:2 * PAYLOAD, P * h:P * (h + 1)],
                                               pay(slot)[:, 2 * PAYLOAD * h:2 * PAYLOAD * (h + 1)], ident[:, :])
                last.then_inc(s_tr, 1)

            def products(i, k):
                b = k % 2
                tile = msg_of(pe, i, k)
                pe.wait_ge(s_ct, i * 4 + (k + 1))
                pe.wait_ge(s_add, i * 4 + (k + 1))
                for c in range(4):
                    o = bank(4 + 3 * b)[:, P * c:P * (c + 1)]
                    if c % 2 == 0:
                        mm(bank(4 + 3 * b)[:, P * c:P * (c + 2)], pair_of("et", b, 2 * P)[0:2 * PAYLOAD, P * (c // 2):P * (c // 2 + 1)],
                           w_edge, start=True, stop=False)
                    for part in range(3):
                        last = mm(o, pair_of("oht", b, 512)[:, P * c:P * (c + 1)],
                                  M["p3"][:, ds(tile * (3 * P) + P * part, P)], start=False,
                                  stop=(c % 2 == 1 and part == 2))
                last.then_inc(s_z, 1)

            def scatter(i, k):
                b, slot = k % 2, k % 4
                tile = msg_of(pe, i, k)
                pe.wait_ge(s_m3, i * 4 + (k + 1))
                for c in range(4):
                    for part in ("m1", "m2", "m3"):
                        last = mm(ps[:, ds(tile * FEAT, FEAT)], M["oh"][:, 512 * slot + P * c:512 * slot + P * (c + 1)],
                                  pair_of(part, b, 256)[:, FEAT * c:FEAT * (c + 1)], start=False, stop=False)
                last.then_inc(s_sc, 1)

            turn(0, 0)
            products(0, 0)
            turn(0, 1)
            products(0, 1)
            turn(0, 2)
            whole = (SPANS - 3) // 4
            with pe.Fori(0, whole) as i:
                for k in range(4):
                    products(i, k + 2)
                    turn(i, k + 3)
                    scatter(i, k)
            for k in range(SPANS - 4 * whole):
                if 4 * whole + k + 2 < SPANS:
                    products(whole, k + 2)
                if 4 * whole + k + 3 < SPANS:
                    turn(whole, k + 3)
                scatter(whole, k)
            for k in range(4):
                last = mm(ps[:, 512 * k:512 * k + 1], M["zeros"][:, 0:P], M["zeros"][:, 0:1], start=False, stop=True)
            last.then_inc(s_tile, 1)
            msg = M["msg"].rearrange("p (t f) -> p t f", f=FEAT)
            pe.wait_ge(s_msg, 1)
            for t in range(TILES):
                last = mm(bank(6, FEAT), ones[:, :], msg[:, t, :], start=(t == 0), stop=(t == TILES - 1))
            last.then_inc(s_sum, 1)
            pe.wait_ge(s_sq, 1)
            for t in range(TILES):
                rows = P if t < TILES - 1 else LAST
                last = mm(bank(7, FEAT), ones[0:rows, :], ts[0:rows, t, :], start=(t == 0), stop=(t == TILES - 1))
            last.then_inc(s_sqs, 1)


def kernel(x, src, dst, edge_attr_16, edge_attr_32, L0_gnn_W_l, L0_gnn_b_l, L0_gnn_W_r, L0_gnn_W_e, L0_gnn_b_e,
           L1_gnn_W, L1_gnn_b, L2_gnn_weights, L3_gnn_W_f, L3_gnn_b_f, L3_gnn_W_s, L3_gnn_b_s, L3_gnn_gamma,
           L3_gnn_beta):
    import numpy as np
    import concourse.bacc as bacc
    from concourse.bass_utils import run_bass_kernel_spmd

    def padded(a, size, value):
        a = np.asarray(a)
        wide = np.full((size,) + a.shape[1:], value, a.dtype)
        wide[:a.shape[0]] = a
        return wide

    src_rows = padded(src, CHUNKS * P, PAD).reshape(CHUNKS, P)
    dst_rows = padded(dst, CHUNKS * P, PAD).reshape(CHUNKS, P)
    row = lambda a: np.asarray(a).reshape(1, FEAT)
    w2 = np.asarray(L2_gnn_weights)
    arrays = {
        "x": padded(x, NPAD, 0),
        "src_cols": src_rows.T, "dst_cols": dst_rows.T, "dst_rows": dst_rows,
        "e16": edge_attr_16, "e32": padded(edge_attr_32, CHUNKS * P, 0),
        "sage_wl": L0_gnn_W_l, "sage_bl": row(L0_gnn_b_l), "sage_wr": L0_gnn_W_r, "sage_we": L0_gnn_W_e,
        "sage_be": row(L0_gnn_b_e), "gcn_w": L1_gnn_W, "gcn_b": row(L1_gnn_b),
        "mean_wt": w2.transpose(0, 2, 1).reshape(3 * FEAT, FEAT),
        "wf": L3_gnn_W_f, "bf": row(L3_gnn_b_f), "ws": L3_gnn_W_s, "bs": row(L3_gnn_b_s),
        "gamma": row(L3_gnn_gamma), "beta": row(L3_gnn_beta),
    }
    arrays = {f"in_{k}": np.ascontiguousarray(a) for k, a in arrays.items()}
    nc = bacc.Bacc("TRN2", target_bir_lowering=False, num_devices=1)
    args = [nc.dram_tensor(k, a.shape, mybir.dt.from_np(a.dtype), kind="ExternalInput").ap()
            for k, a in arrays.items()]
    args.append(nc.dram_tensor("out_x", (N_NODES, FEAT), mybir.dt.float32, kind="ExternalOutput").ap())
    gnn_program(nc, *args)
    result = run_bass_kernel_spmd(nc, [arrays], core_ids=[0])
    return result.results[0]["out_x"]
```

```python
import concourse.bass as bass
from concourse import mybir
from concourse.bass import ds
from contextlib import ExitStack

N_NODES = 3125
FEAT = 64
N_EDGES = 103125
P = 128
TILES = -(-N_NODES // P)
NPAD = TILES * P
LAST = N_NODES - (TILES - 1) * P
CHUNKS = -(-N_EDGES // (8 * P)) * 8
PAIRS = CHUNKS // 2
QUADS = CHUNKS // 4
CPR = 8
BOUND_ROWS = CHUNKS // CPR
EDGE_F = 32
EDGE_D = 16
LAYERS = 5
GROUPS = -(-TILES // 4)
ECAT = EDGE_D + 2
PAD = 4095
WIN = 64
WINDOWS = NPAD // WIN
RUN = 10
MOV = TILES * WIN
BLOCK = 8
SPAN = 512
SPANS = (N_EDGES + TILES * (SPAN - 1)) // SPAN
TABLE = SPANS * SPAN
PAYLOAD = EDGE_F + 2
MOVED = -(-N_EDGES // P)
BATCH = 13
EARLY = 5
FILL = 8
ARENA = 18600


def gnn_program(nc, x, src_cols, dst_cols, dst_rows, e16, e32, sage_wl, sage_bl, sage_wr, sage_we,
                sage_be, gcn_w, gcn_b, mean_wt, wf, bf_, ws, bs_, gamma, beta, out):
    f32, bf16, i32, i16 = mybir.dt.float32, mybir.dt.bfloat16, mybir.dt.int32, mybir.dt.int16
    ALU, ACT, AX = mybir.AluOpType, mybir.ActivationFunctionType, mybir.AxisListType

    table_e = nc.dram_tensor("table_e", [TABLE + P, PAYLOAD], f32, kind="Internal").ap()
    table_q = nc.dram_tensor("table_q", [NPAD, 2 * FEAT], f32, kind="Internal").ap()

    with ExitStack() as ctx:
        def sb(name, shape, dt):
            return ctx.enter_context(nc.sbuf_tensor(name, shape, dt))

        def sem(name):
            return ctx.enter_context(nc.semaphore(name))

        adj = sb("adj", [P, TILES * NPAD], bf16)
        arena = sb("arena", [P, ARENA], bf16)
        A3 = adj[:, :].rearrange("p (k d) -> p k d", k=TILES)

        def views(base, wanted, limit):
            found, at = {}, 0
            for name, words, dt in wanted:
                v = base[:, at:at + 2 * words]
                found[name] = v if dt == bf16 else v.bitcast(dt)
                at += 2 * words
            assert at <= limit, at
            return found

        B = views(arena, [("iota", MOV // 2, i16), ("key_lo", CHUNKS, f32), ("key_mv", CHUNKS, f32),
                          ("oh_lo", 2 * P, bf16), ("oh_mv", 2 * MOV, bf16), ("edge_at", CHUNKS, i32),
                          ("ends", CHUNKS, i16), ("payload", 2 * BATCH * PAYLOAD, f32), ("moving", 2 * BATCH, i32),
                          ("wgrid", 3 * WINDOWS, f32), ("iota_f", P, f32),
                          ("lo_base", 2 * P, f32), ("lo_far", 2 * P, bf16)], ARENA)
        E = views(B["oh_mv"], [("tmp_i", P, i32), ("bounds", 2 * CPR, f32), ("row", 5 * WINDOWS, f32),
                               ("fill", FILL * PAYLOAD, f32), ("before", P, f32)], 4 * MOV)
        tmp_i, bounds = E["tmp_i"], E["bounds"]
        row = E["row"][0:1, :].rearrange("p (k w) -> p k w", k=5)
        wgrid = B["wgrid"].rearrange("p (k w) -> p k w", k=3)
        payload = B["payload"].rearrange("p (b c w) -> p b c w", b=2, c=BATCH)
        ends = B["ends"].rearrange("p (c w) -> p c w", w=2)
        oh_lo = B["oh_lo"].rearrange("p (s n) -> p s n", s=4)
        oh_mv = B["oh_mv"].rearrange("p (s n) -> p s n", s=4)
        lo_far = B["lo_far"].rearrange("p (s n) -> p s n", s=4)
        S = views(adj, [("src_i", CHUNKS, i32), ("dst_i", CHUNKS, i32), ("ka", CHUNKS, i32), ("kb", CHUNKS, i32),
                        ("bound_dst", CPR * P, i32), ("dlo", CHUNKS, f32), ("dhi", CHUNKS, i32),
                        ("oh_dhi", BLOCK * WINDOWS, bf16), ("oh_dlo", BLOCK * WIN, bf16), ("half_no", WINDOWS, i32),
                        ("seen", PAIRS * TILES // 2, bf16), ("seen_at", PAIRS * TILES, f32),
                        ("rows", TILES * 256, i32), ("pair_no", PAIRS, i32), ("edge_no", 256, i32),
                        ("node_no", TILES, i32), ("win_i", 3 * WINDOWS, i32),
                        ("hit", CPR * 2 * WINDOWS, f32)], TILES * NPAD)
        hit = S["hit"].rearrange("p (q a w) -> p q a w", q=CPR, a=2)
        R = views(S["seen"], [("tile_f", CHUNKS, f32), ("rank", CHUNKS, f32),
                              ("at", CHUNKS, f32), ("counts", TILES, f32), ("spans", TILES, f32),
                              ("spans_i", TILES, i32), ("base", TILES, f32), ("upto", TILES, f32),
                              ("dump_i", 1, i32), ("dump", 1, f32)], PAIRS * TILES)
        oh_tile = S["seen_at"].bitcast(bf16).rearrange("p (t c) -> p t c", t=TILES)
        L = views(arena, [("x", TILES * FEAT, f32), ("h", TILES * FEAT, f32), ("t", TILES * FEAT, f32),
                          ("y12", TILES * FEAT, bf16), ("y3", TILES * 33, bf16),
                          ("t12", 1024, f32), ("t3", 1024, f32)], ARENA)
        xs, hs, ts = (L[k].rearrange("p (t f) -> p t f", f=FEAT) for k in ("x", "h", "t"))
        y12 = L["y12"].rearrange("p (t f) -> p t f", f=2 * FEAT)
        y3 = L["y3"].rearrange("p (t f) -> p t f", f=66)
        t12 = L["t12"].rearrange("p (s n) -> p s n", s=2)
        t3 = L["t3"].rearrange("p (s n) -> p s n", s=2)
        M = views(adj, [("p3", TILES * 3 * FEAT, bf16), ("lane", P, f32),
                        ("lane_i", P, i32), ("pay", 4 * 4 * PAYLOAD, f32), ("now", 16, i32), ("gq", 2 * 512, f32),
                        ("oh", 4 * 256, bf16), ("oht", 2 * 256, bf16), ("et", 4 * P, f32), ("w_edge", 2 * P, f32), ("z", 2 * 512, f32),
                        ("ab", 2 * 512, f32), ("ln", 2 * 512, f32), ("gate", 2 * 256, f32), ("val", 2 * 256, f32),
                        ("hm", 256, f32), ("m1", 256, bf16), ("m2", 256, bf16), ("m3", 256, bf16),
                        ("msg", TILES * FEAT, f32), ("pq", TILES * 256, f32), ("zeros", 256, bf16),
                        ("span_no", SPANS, i32), ("is_upto", SPANS * TILES, f32), ("tile_f", SPANS, f32),
                        ("tile_of", SPANS, i32)], TILES * NPAD)

        pq = M["pq"].rearrange("p (t w) -> p t w", t=TILES)
        w_edge = M["w_edge"][0:2 * PAYLOAD, :]
        ident = sb("ident", [P, P], f32)
        ident16 = sb("ident16", [P, P], bf16)
        zeros = sb("zeros", [P, P], bf16)
        ones = sb("ones", [P, P], f32)
        last_pair = sb("last_pair", [P, TILES], f32)
        cnt = sb("cnt", [P, TILES], f32)
        scale = sb("scale", [P, 3, TILES], f32)
        stat = sb("stat", [P, 3, TILES], f32)
        gat_i = sb("gat_i", [P, TILES], i32)
        gat_e = sb("gat_e", [P, TILES], i32)
        w12 = sb("w12", [P, LAYERS, 65], f32)
        w3 = sb("w3", [65, LAYERS, 65], f32)
        wroot = sb("wroot", [FEAT, FEAT], f32)
        wlast = sb("wlast", [ECAT, FEAT], f32)
        wpq = sb("wpq", [FEAT + 1, 4 * FEAT], f32)
        ecat = sb("ecat", [P, TILES, ECAT], f32)
        vecs = sb("vecs", [P, 3, FEAT], f32)
        span0 = sb("span0", [P, TILES], f32)
        pnum = sb("pnum", [P, 2, CPR], f32)
        ext = sb("ext", [WINDOWS, 2], f32)
        ext4 = sb("ext4", [WINDOWS, 4], f32)
        trip = sb("trip", [1, 3, WINDOWS], i32)
        pnum_i = sb("pnum_i", [P, 2 * CPR], i32)
        bn = sb("bn", [P, 3, FEAT], f32)

        ps = ctx.enter_context(nc.psum_tensor("ps", [P, 8 * 512], f32))

        def bank(b, n=512):
            return ps[:, 512 * b:512 * b + n]

        adj_acc = [ps[:, 0:MOV], ps[:, 2048:2048 + MOV]]

        s_const = sem("s_const"); s_in = sem("s_in"); s_pair = sem("s_pair"); s_wz = sem("s_wz"); s_w = sem("s_w")
        s_ch = sem("s_ch")
        s_hit = sem("s_hit"); s_hitT = sem("s_hitT"); s_ext = sem("s_ext"); s_extT = sem("s_extT")
        s_fs = sem("s_fs"); s_fill = sem("s_fill"); s_tiles = sem("s_tiles"); s_counts = sem("s_counts")
        s_pre = sem("s_pre"); s_place = sem("s_place")
        s_e32 = [sem(f"s_e32_{b}") for b in range(2)]; s_ids = sem("s_ids")
        s_moved = [sem(f"s_moved{b}") for b in range(2)]; s_go = sem("s_go")
        s_seen_o = sem("s_seen_o"); s_seen_c = sem("s_seen_c"); s_seen_a = sem("s_seen_a"); s_lp = sem("s_lp")
        s_rows = sem("s_rows"); s_gat = sem("s_gat"); s_e16 = sem("s_e16")
        s_ready = sem("s_ready"); s_oh = sem("s_oh"); s_base = sem("s_base"); s_far = sem("s_far"); s_lo = sem("s_lo")
        s_chunk = sem("s_chunk"); s_win = sem("s_win"); s_adj = sem("s_adj")
        s_x = sem("s_x"); s_var = sem("s_var"); s_std = sem("s_std"); s_y = sem("s_y"); s_y3 = sem("s_y3")
        s_agg = sem("s_agg"); s_t12 = sem("s_t12"); s_t3 = sem("s_t3"); s_proj = sem("s_proj"); s_used = sem("s_used")
        s_cat = sem("s_cat"); s_catT = sem("s_catT"); s_catS = sem("s_catS"); s_catO = sem("s_catO")
        s_catU = sem("s_catU")
        s_pq = sem("s_pq"); s_pf = sem("s_pf"); s_pa = sem("s_pa"); s_io3 = sem("s_io3"); s_p3 = sem("s_p3")
        s_wb0 = sem("s_wb0"); s_wb = sem("s_wb")
        s_pay = [sem(f"s_pay{b}") for b in range(4)]; s_now = sem("s_now"); s_g = [sem(f"s_g{b}") for b in range(2)]
        s_oh3 = sem("s_oh3"); s_tr = sem("s_tr"); s_ct = sem("s_ct"); s_z = sem("s_z"); s_add = sem("s_add")
        s_ab = sem("s_ab"); s_ex = sem("s_ex"); s_ln = sem("s_ln"); s_ga = sem("s_ga"); s_gt = sem("s_gt")
        s_hm = sem("s_hm"); s_m1 = sem("s_m1"); s_r1 = sem("s_r1"); s_m2 = sem("s_m2"); s_m3 = sem("s_m3")
        s_sc = sem("s_sc")
        s_tile = sem("s_tile"); s_msg = sem("s_msg"); s_sum = sem("s_sum"); s_sq = sem("s_sq"); s_sqs = sem("s_sqs")
        s_bnv = sem("s_bnv"); s_bns = sem("s_bns"); s_fin = sem("s_fin"); s_out = sem("s_out")

        block = ctx.enter_context(nc.Block())

        def trip_value(eng, t, part):
            least, most = ((0, CHUNKS - 12), (3, QUADS), (0, QUADS * WINDOWS))[part]
            return eng.value_load(trip[0:1, part, ds(t, 1)], min_val=least, max_val=most)

        def window_trip(eng, t):
            return [trip_value(eng, t, part) for part in range(3)]

        def chunk_of(first, j, a):
            c = nc.s_assert_within(first + j * 4 + a, 0, CHUNKS - 1,
                                   skip_runtime_bounds_check_because="a window's chunks end at the last chunk")
            return ds(c, 1)

        def pair_of(name, b, n):
            return M[name][:, n * b:n * (b + 1)]

        def pay(slot):
            return M["pay"][:, 4 * PAYLOAD * slot:4 * PAYLOAD * (slot + 1)]

        def pay_of(slot):
            return pay(slot).rearrange("p (c w) -> p c w", c=4)

        def group_tile(eng, i, k):
            return eng.value_load(M["tile_of"][0:1, ds(i * 4 + k, 1)], min_val=0, max_val=TILES - 1)

        n_weights = 0

        @block.sync
        def _(sp):
            nonlocal n_weights
            sp.dma_start(S["dst_i"], dst_cols).then_inc(s_in, 16)
            sp.dma_start(S["src_i"], src_cols).then_inc(s_in, 16)
            sp.dma_start(S["bound_dst"][0:BOUND_ROWS, :],
                         dst_rows.rearrange("(r q) e -> r (q e)", r=BOUND_ROWS)).then_inc(s_pair, 16)
            sp.wait_ge(s_fs, 1)
            reps = TABLE // (P * FILL)
            sp.dma_start(table_e[0:TABLE, :].rearrange("(p n r) w -> p n (r w)", p=P, r=FILL),
                         E["fill"].unsqueeze(1).broadcast_to([P, reps, FILL * PAYLOAD])).then_inc(s_fill, 16)
            sp.wait_ge(s_wz, 1)
            w_list = [sage_wl, gcn_w] + [mean_wt[64 * l:64 * (l + 1), :] for l in range(3)]
            moves = []
            for l, w in enumerate(w_list):
                moves += [(w12[0:64, l, 0:64], w), (w12[64:128, l, 0:64], w), (w3[0:64, l, 0:64], w)]
            moves += [(wroot[:, :], sage_wr), (wlast[0:16, :], sage_we), (wlast[16:17, :], sage_be),
                      (wlast[17:18, :], sage_bl)]
            for k, (w, b_row) in enumerate(((wf, bf_), (ws, bs_))):
                moves += [(wpq[0:64, 64 * k:64 * (k + 1)], w[0:64, :]),
                          (wpq[0:64, 128 + 64 * k:128 + 64 * (k + 1)], w[64:128, :]),
                          (wpq[64:65, 128 + 64 * k:128 + 64 * (k + 1)], b_row)]
            for k, v in enumerate((gcn_b, gamma, beta)):
                moves.append((vecs[:, k, :], v.rearrange("o f -> (o f)").partition_broadcast(P)))
            for to, of in moves:
                sp.dma_start(to, of).then_inc(s_w, 16)
            n_weights = len(moves)
            e32_chunks = e32.rearrange("(c p) w -> p c w", p=P)
            for b in range(2):
                sp.dma_start(payload[:, b, :, 0:EDGE_F], e32_chunks[:, BATCH * b:BATCH * (b + 1), :]).then_inc(s_e32[b], 16)
            with sp.Fori(1, MOVED // (2 * BATCH)) as i:
                for b in range(2):
                    sp.wait_ge(s_moved[b], i * (16 * BATCH))
                    sp.dma_start(payload[:, b, :, 0:EDGE_F],
                                 e32_chunks[:, ds(i * (2 * BATCH) + BATCH * b, BATCH), :]).then_inc(s_e32[b], 16)
            sp.wait_ge(s_adj, WINDOWS + 2)
            for b in range(2):
                sp.wait_ge(s_moved[b], 16 * BATCH * (MOVED // (2 * BATCH)))
            sp.dma_start(xs, x.rearrange("(t p) f -> p t f", p=P)).then_inc(s_x, 16)
            sp.wait_ge(s_wb0, 1)
            for c in range(2):
                for k, w in enumerate((wf, ws)):
                    sp.dma_start(w_edge[PAYLOAD * c:PAYLOAD * c + EDGE_F, P * c + FEAT * k:P * c + FEAT * (k + 1)],
                                 w[2 * FEAT:2 * FEAT + EDGE_F, :]).then_inc(s_wb, 16)
            rows_q = table_q.rearrange("(t p) w -> p t w", p=P)
            for t in range(0, TILES, 5):
                sp.wait_ge(s_catU, GROUPS + t + 5)
                sp.dma_start(rows_q[:, t:t + 5, :], pq[:, t:t + 5, P:2 * P]).then_inc(s_pq, 16)
            groups = table_e[0:TABLE, :].rearrange("(r c) w -> r (c w)", c=4)

            def load(i, k):
                sp.wait_ge(s_tr, i * 4 + (k + 1))
                sp.wait_ge(s_now, i * 4 + (k + 1))
                sp.dma_start(pay(k), groups[ds(i * (4 * P) + P * k, P), :]).then_inc(s_pay[k], 16)

            with sp.Fori(0, SPANS // 4) as i:
                for k in range(4):
                    load(i, k)
            for k in range(SPANS % 4):
                load(SPANS // 4, k)
            sp.wait_ge(s_fin, 1)
            full = (TILES - 1) * P
            sp.dma_start(out[0:full, :].rearrange("(t p) f -> p t f", p=P), xs[:, 0:TILES - 1, :]).then_inc(s_out, 16)
            sp.dma_start(out[full:N_NODES, :], xs[0:LAST, TILES - 1, :]).then_inc(s_out, 16)
            sp.wait_ge(s_out, 32)

        @block.gpsimd
        def _(pool):
            g = nc.gpsimd
            g.iota(tmp_i[:], pattern=[[1, P]], base=0, channel_multiplier=-1)
            g.iota(B["iota"], pattern=[[1, MOV]], base=0, channel_multiplier=0)
            g.iota(S["win_i"][:, 0:WINDOWS], pattern=[[WIN, WINDOWS]], base=0, channel_multiplier=0)
            g.iota(S["win_i"][:, WINDOWS:2 * WINDOWS], pattern=[[WIN, WINDOWS]], base=WIN, channel_multiplier=0)
            g.iota(S["win_i"][:, 2 * WINDOWS:3 * WINDOWS], pattern=[[P, WINDOWS]], base=0, channel_multiplier=0)
            g.iota(pnum_i[:, 0:CPR], pattern=[[1, CPR]], base=1, channel_multiplier=CPR)
            g.iota(pnum_i[:, CPR:2 * CPR], pattern=[[-1, CPR]], base=CHUNKS, channel_multiplier=-CPR)
            g.iota(S["half_no"].rearrange("p (h t) -> p h t", h=2), pattern=[[1, 2], [2, TILES]], base=0,
                   channel_multiplier=0)
            g.iota(S["node_no"], pattern=[[P, TILES]], base=0, channel_multiplier=1)
            g.iota(R["dump_i"], pattern=[[1, 1]], base=TABLE, channel_multiplier=1)
            g.iota(S["edge_no"], pattern=[[1, 256]], base=1, channel_multiplier=0)
            g.iota(S["pair_no"], pattern=[[1, PAIRS]], base=1, channel_multiplier=0).then_inc(s_const, 1)
            pool.wait_ge(s_place, 1)
            pool.wait_ge(s_fill, 16)

            def move(lo, hi):
                with pool.Fori(lo, hi) as i:
                    for b in range(2):
                        batch = ds(i * (2 * BATCH) + BATCH * b, BATCH)
                        pool.wait_ge(s_e32[b], i * 16 + 16)
                        pool.sem_inc(s_go, 1)
                        g.tensor_copy(payload[:, b, :, EDGE_F:PAYLOAD], ends[:, batch, :])
                        g.tensor_copy(B["moving"][:, BATCH * b:BATCH * (b + 1)], B["edge_at"][:, batch]).then_inc(s_ids, 1)
                        pool.wait_ge(s_ids, i * 2 + (b + 1))
                        pool.sem_inc(s_go, 1)
                        for c in range(BATCH):
                            at = B["moving"][:, BATCH * b + c:BATCH * b + c + 1]
                            g.indirect_dma_start(out=table_e, out_offset=bass.IndirectOffsetOnAxis(ap=at, axis=0),
                                                 in_=payload[:, b, c, :], in_offset=None).then_inc(s_moved[b], 16)

            move(0, EARLY)
            pool.wait_ge(s_lp, 1)
            pair_rows = dst_rows.rearrange("(r a) e -> r (a e)", a=2)
            for t in range(TILES):
                g.indirect_dma_start(out=S["rows"][:, 256 * t:256 * (t + 1)], out_offset=None, in_=pair_rows,
                                     in_offset=bass.IndirectOffsetOnAxis(ap=gat_i[:, t:t + 1], axis=0)
                                     ).then_inc(s_rows, 16)
            pool.wait_ge(s_gat, 1)
            for t in range(TILES):
                g.indirect_dma_start(out=ecat[:, t, 0:EDGE_D], out_offset=None, in_=e16,
                                     in_offset=bass.IndirectOffsetOnAxis(ap=gat_e[:, t:t + 1], axis=0)
                                     ).then_inc(s_e16, 16)
            move(EARLY, MOVED // (2 * BATCH))
            pool.wait_ge(s_used, LAYERS * GROUPS + 2)
            g.iota(M["lane_i"], pattern=[[1, P]], base=0, channel_multiplier=0)
            g.iota(M["span_no"], pattern=[[1, SPANS]], base=0, channel_multiplier=0).then_inc(s_io3, 1)
            pool.wait_ge(s_pq, 16 * (TILES // 5))
            pool.sem_inc(s_now, 4)

            def indices(i, k):
                pool.wait_ge(s_pay[k % 4], (i + k // 4) * 16 + 16)
                pool.sem_inc(s_go, 1)
                g.tensor_copy(M["now"][:, 4 * (k % 4):4 * (k % 4) + 4], pay_of(k % 4)[:, :, PAYLOAD - 1]).then_inc(s_now, 1)

            def gather(i, k):
                pool.wait_ge(s_now, i * 4 + (k + 5))
                pool.wait_ge(s_add, i * 4 + (k + 1))
                pool.sem_inc(s_go, 1)
                for c in range(4):
                    at = M["now"][:, 4 * (k % 4) + c:4 * (k % 4) + c + 1]
                    g.indirect_dma_start(out=pair_of("gq", k % 2, 512)[:, P * c:P * (c + 1)], out_offset=None,
                                         in_=table_q, in_offset=bass.IndirectOffsetOnAxis(ap=at, axis=0)
                                         ).then_inc(s_g[k % 2], 16)

            indices(0, 0)
            with pool.Fori(0, SPANS // 4) as i:
                for k in range(4):
                    indices(i, k + 1)
                    gather(i, k)
            indices(SPANS // 4, 1)
            gather(SPANS // 4, 0)
            gather(SPANS // 4, 1)

        @block.vector
        def _(v):
            dve = nc.vector
            chain = [0]

            def link(ins):
                chain[0] += 1
                ins.then_inc(s_ch, 1)
                v.wait_ge(s_ch, chain[0])

            dve.memset(w12[:], 0.0)
            dve.memset(wpq[64:65, :], 0.0)
            link(dve.memset(w3[:], 0.0))
            dve.memset(w3[64:65, :, 64:65], 1.0).then_inc(s_wz, 1)
            fill = E["fill"].rearrange("p (r w) -> p r w", r=FILL)
            link(dve.memset(E["fill"], 0.0))
            dve.memset(fill[:, :, EDGE_F:EDGE_F + 1], float(PAD)).then_inc(s_fs, 1)
            dve.memset(ones[:], 1.0)
            dve.memset(zeros[:], 0.0)
            v.wait_ge(s_const, 1)
            dve.tensor_scalar(ident[:], tmp_i[:], 0.0, None, ALU.is_equal)
            dve.tensor_scalar(ident16[:], tmp_i[:], 0.0, None, ALU.is_equal)
            dve.tensor_copy(wgrid[:, :, :], S["win_i"].rearrange("p (a w) -> p a w", a=3))
            link(dve.tensor_copy(pnum[:, :, :], pnum_i[:, :].rearrange("p (a t) -> p a t", a=2)))
            v.wait_ge(s_pair, 16)
            r = slice(0, BOUND_ROWS)
            pd = S["bound_dst"][r, :].rearrange("p (q e) -> p q e", q=CPR)
            dve.tensor_reduce(bounds[r, 0:CPR], pd, AX.X, ALU.min)
            link(dve.tensor_reduce(bounds[r, CPR:2 * CPR], pd, AX.X, ALU.max))
            for q in range(CPR):
                dve.tensor_scalar(hit[r, q, 0, :], wgrid[r, 0, :], bounds[r, CPR + q:CPR + q + 1], None, ALU.is_le).then_inc(s_ch, 1)
            chain[0] += CPR
            v.wait_ge(s_ch, chain[0])
            for q in range(CPR):
                dve.scalar_tensor_tensor(hit[r, q, 0, :], wgrid[r, 1, :], bounds[r, q:q + 1], hit[r, q, 0, :],
                                         ALU.is_gt, ALU.mult).then_inc(s_ch, 1)
            chain[0] += CPR
            v.wait_ge(s_ch, chain[0])
            for q in range(CPR):
                dve.tensor_scalar(hit[r, q, 1, :], hit[r, q, 0, :], pnum[r, 0, q:q + 1], None, ALU.mult).then_inc(s_ch, 1)
            chain[0] += CPR
            v.wait_ge(s_ch, chain[0])
            for q in range(CPR):
                last = dve.tensor_scalar(hit[r, q, 0, :], hit[r, q, 0, :], pnum[r, 1, q:q + 1], None, ALU.mult)
            last.then_inc(s_hit, 1)
            v.wait_ge(s_in, 32)
            src_i, dst_i, ka, kb = S["src_i"], S["dst_i"], S["ka"], S["kb"]
            dve.tensor_scalar(ka, dst_i, 6, 7, ALU.logical_shift_right, ALU.logical_shift_left)
            link(dve.tensor_scalar(kb, src_i, P - 1, None, ALU.bitwise_and))
            link(dve.tensor_tensor(B["key_lo"], ka, kb, ALU.add))
            dve.tensor_scalar(ka, src_i, 7, 6, ALU.logical_shift_right, ALU.logical_shift_left)
            link(dve.tensor_scalar(kb, dst_i, WIN - 1, None, ALU.bitwise_and))
            link(dve.tensor_tensor(B["key_mv"], ka, kb, ALU.add))
            dve.tensor_scalar(S["dhi"], dst_i, 6, None, ALU.logical_shift_right)
            dve.tensor_copy(S["dlo"], kb).then_inc(s_ch, 1)
            chain[0] += 1
            v.wait_ge(s_ch, chain[0])
            v.wait_ge(s_hitT, 1)
            half = CPR // 2 * BOUND_ROWS
            for a in range(2):
                dve.tensor_reduce(ext4[:, 2 * a:2 * a + 2],
                                  ps[0:WINDOWS, 1024 * a:1024 * (a + 1)].rearrange("p (h n) -> p h n", h=2)[:, :, 0:half],
                                  AX.X, ALU.max).then_inc(s_ch, 1)
            chain[0] += 2
            v.wait_ge(s_ch, chain[0])
            dve.tensor_reduce(ext[:, :], ext4[:, :].rearrange("p (a h) -> p a h", a=2), AX.X, ALU.max).then_inc(s_ext, 1)
            v.wait_ge(s_extT, 1)
            er = ps[0:1, 2048:2048 + 2 * WINDOWS]
            link(dve.memset(row[:, 4, :], 0.0))
            link(dve.tensor_scalar(row[:, 0, :], er[:, 0:WINDOWS], -1.0, float(CHUNKS), ALU.mult, ALU.add))
            link(dve.tensor_tensor(row[:, 1, :], er[:, WINDOWS:2 * WINDOWS], row[:, 0, :], ALU.subtract))
            link(dve.tensor_scalar(row[:, 1, :], row[:, 1, :], 9.0, 3.0, ALU.max, ALU.add))
            link(dve.tensor_copy(trip[:, 1, :], row[:, 1, :]))
            link(dve.tensor_scalar(trip[:, 1, :], trip[:, 1, :], 2, None, ALU.logical_shift_right))
            link(dve.tensor_copy(row[:, 1, :], trip[:, 1, :]))
            link(dve.tensor_scalar(row[:, 3, :], row[:, 1, :], -4.0, float(CHUNKS), ALU.mult, ALU.add))
            link(dve.tensor_tensor(row[:, 0, :], row[:, 0, :], row[:, 3, :], ALU.min))
            link(dve.tensor_tensor_scan(row[:, 2, :], row[:, 1, :], row[:, 4, :], 0.0, ALU.add, ALU.add))
            link(dve.tensor_tensor(row[:, 3, :], row[:, 2, :], row[:, 1, :], ALU.subtract))
            dve.tensor_copy(trip[:, 0, :], row[:, 0, :])
            link(dve.tensor_copy(trip[:, 2, :], row[:, 3, :]))
            link(dve.tensor_scalar(E["before"], tmp_i[:], 0.0, None, ALU.is_gt))
            link(dve.tensor_scalar(kb, src_i, 7, None, ALU.logical_shift_right))
            dve.tensor_copy(R["dump"], R["dump_i"])
            link(dve.tensor_copy(R["tile_f"], kb))
            for t in range(TILES):
                dve.tensor_scalar(oh_tile[:, t, :], R["tile_f"], float(t), None, ALU.is_equal).then_inc(s_tiles, 1)
            link(dve.tensor_scalar(kb, src_i, P - 1, None, ALU.bitwise_and))
            dve.tensor_copy(ends[:, :, 0], kb)
            dve.tensor_copy(ends[:, :, 1], dst_i)
            v.wait_ge(s_pre, 1)
            total, earlier = bank(3)[:, 0:TILES], bank(3)[:, 64:64 + TILES]
            link(dve.tensor_scalar(R["spans"], total, float(SPAN - 1), None, ALU.add))
            link(dve.tensor_copy(R["spans_i"], R["spans"]))
            link(dve.tensor_scalar(R["spans_i"], R["spans_i"], 9, None, ALU.logical_shift_right))
            link(dve.tensor_copy(R["spans"], R["spans_i"]))
            link(dve.tensor_scalar(R["spans"], R["spans"], 1.0, None, ALU.max))
            link(dve.tensor_tensor_scan(R["upto"], R["spans"], ones[:, 0:TILES], 0.0, ALU.add, ALU.mult))
            link(dve.tensor_tensor(span0[:], R["upto"], R["spans"], ALU.subtract))
            link(dve.tensor_scalar(R["base"], span0[:], float(SPAN), -1.0, ALU.mult, ALU.add))
            link(dve.tensor_tensor(R["base"], R["base"], earlier, ALU.add))
            link(dve.memset(R["at"], 0.0))
            end = slice(MOVED - 1, MOVED)
            link(dve.tensor_scalar(R["at"][:, end], R["tile_f"][:, end], float(PAD >> 7), R["dump"], ALU.is_equal, ALU.mult))
            rank, at = R["rank"], R["at"]
            every = ones[:, 0:1].broadcast_to([P, CHUNKS])
            for t in range(TILES):
                link(dve.tensor_tensor_scan(rank, oh_tile[:, t, :], every, R["base"][:, t:t + 1], ALU.add, ALU.mult))
                link(dve.copy_predicated(at, oh_tile[:, t, :].bitcast(i16), rank))
            dve.tensor_copy(B["edge_at"], at).then_inc(s_place, 1)
            v.wait_ge(s_place, 1)
            dlo2, dhi2 = (S[k].rearrange("p (b c n) -> p b c n", b=2, c=BLOCK) for k in ("oh_dlo", "oh_dhi"))

            def destination_rows(u, b):
                v.wait_ge(s_seen_c, u + 1)
                chunks = ds(u * BLOCK, BLOCK)
                for to, number, key, n in ((dlo2, B["iota"], S["dlo"], WIN), (dhi2, S["half_no"], S["dhi"], WINDOWS)):
                    big = [P, BLOCK, n]
                    last = dve.tensor_tensor(to[:, b, :, :], number[:, 0:n].unsqueeze(1).broadcast_to(big),
                                             key[:, chunks].unsqueeze(2).broadcast_to(big), ALU.is_equal)
                last.then_inc(s_seen_o, 1)

            v.sem_inc(s_seen_c, 2)
            with v.Fori(0, CHUNKS // (2 * BLOCK)) as i:
                for b in range(2):
                    destination_rows(i * 2 + b, b)
            destination_rows(CHUNKS // BLOCK - 1, 0)
            v.wait_ge(s_seen_a, CHUNKS // BLOCK + 2)
            big = [P, PAIRS, TILES]
            link(dve.scalar_tensor_tensor(
                S["seen_at"].rearrange("p (r t) -> p r t", t=TILES), S["seen"].rearrange("p (r t) -> p r t", t=TILES),
                0.0, S["pair_no"].unsqueeze(2).broadcast_to(big), ALU.is_gt, ALU.mult))
            link(dve.tensor_reduce(last_pair[:], S["seen_at"].rearrange("p (r t) -> p t r", t=TILES), AX.X, ALU.max))
            dve.tensor_scalar(gat_i[:], last_pair[:], -1.0, 0.0, ALU.add, ALU.max).then_inc(s_lp, 1)
            v.wait_ge(s_rows, 16 * TILES)
            rows = S["rows"].rearrange("p (t e) -> p t e", t=TILES)
            big = [P, TILES, 256]
            link(dve.tensor_tensor(rows, rows, S["node_no"].unsqueeze(2).broadcast_to(big), ALU.is_equal))
            link(dve.tensor_tensor(rows, rows, S["edge_no"].unsqueeze(1).broadcast_to(big), ALU.mult))
            link(dve.tensor_reduce(stat[:, 0, :], rows, AX.X, ALU.max))
            link(dve.tensor_scalar(stat[:, 1, :], last_pair[:], 256.0, -257.0, ALU.mult, ALU.add))
            link(dve.tensor_tensor(stat[:, 1, :], stat[:, 1, :], stat[:, 0, :], ALU.add))
            link(dve.tensor_scalar(stat[:, 1, :], stat[:, 1, :], 0.0, None, ALU.max))
            dve.tensor_copy(gat_e[:], stat[:, 1, :]).then_inc(s_gat, 1)
            link(dve.tensor_copy(B["iota_f"], B["iota"][:, 0:P]))
            v.wait_ge(s_gat, 1)
            v.wait_ge(s_fill, 16)
            v.sem_inc(s_ready, 1)

            def window_chunks(w, first, before, j):
                for a in range(4):
                    v.wait_ge(s_chunk, (before + j) * 4 + (a + 1))
                    dve.tensor_scalar(oh_mv[:, a, :], B["iota"], B["key_mv"][:, chunk_of(first, j, a)], None,
                                      ALU.is_equal).then_inc(s_oh, 1)

            with v.Fori(0, WINDOWS // RUN) as i:
                trip_now = window_trip(v, i * RUN)
                for s in range(RUN):
                    w, trip_next = i * RUN + s, []
                    first, count, before = trip_now
                    for j in range(2):
                        window_chunks(w, first, before, j)
                        if s + 1 < RUN:
                            trip_next.append(trip_value(v, w + 1, j))
                    with v.Fori(2, count) as j:
                        window_chunks(w, first, before, j)
                    if s + 1 < RUN:
                        trip_now = trip_next + [trip_value(v, w + 1, 2)]

            v.wait_ge(s_adj, WINDOWS + 2)
            v.wait_ge(s_w, 16 * n_weights)
            link(dve.tensor_scalar(stat[:, 1, :], last_pair[:], 0.0, None, ALU.is_gt))
            dve.memset(ecat[:, :, EDGE_D + 1:ECAT], 1.0)
            link(dve.tensor_copy(ecat[:, :, EDGE_D], stat[:, 1, :]))
            v.wait_ge(s_x, 16)

            wide = [P, TILES, FEAT]

            def over(s):
                return s.unsqueeze(2).broadcast_to(wide)

            n_std = [0]

            def layernorm_relu():
                link(dve.tensor_reduce(stat[:, 0, :], xs, AX.X, ALU.add))
                link(dve.tensor_scalar(stat[:, 0, :], stat[:, 0, :], -1.0 / FEAT, None, ALU.mult))
                link(dve.tensor_tensor(hs, xs, over(stat[:, 0, :]), ALU.add))
                link(dve.tensor_tensor(ts, hs, hs, ALU.mult))
                link(dve.tensor_reduce(stat[:, 1, :], ts, AX.X, ALU.add))
                dve.tensor_scalar(stat[:, 1, :], stat[:, 1, :], 1.0 / FEAT, 1e-5, ALU.mult, ALU.add).then_inc(s_var, 1)
                n_std[0] += 1
                v.wait_ge(s_std, n_std[0])
                link(dve.reciprocal(stat[:, 2, :], stat[:, 2, :]))
                link(dve.tensor_tensor(hs, hs, over(stat[:, 2, :]), ALU.mult))
                link(dve.tensor_scalar(hs, hs, 0.0, None, ALU.max))

            def split_y(y, l):
                link(dve.tensor_copy(y12[:, :, 0:FEAT], y))
                link(dve.tensor_tensor(ts, y, y12[:, :, 0:FEAT], ALU.subtract))
                dve.tensor_copy(y12[:, :, FEAT:2 * FEAT], ts).then_inc(s_y, 1)
                v.wait_ge(s_y, l + 1)
                dve.tensor_tensor(y3[:, :, 0:FEAT], ts, y12[:, :, FEAT:2 * FEAT], ALU.subtract).then_inc(s_y3, 1)

            link(dve.memset(y3[:, :, FEAT:FEAT + 2], 1.0))
            ps3 = [bank(2), bank(3)]
            po = [bank(4), bank(5)]
            for l in range(LAYERS):
                if l in (0, 1, 2):
                    layernorm_relu()
                if l == 0:
                    split_y(hs, l)
                elif l == 1:
                    link(dve.tensor_tensor(ts, hs, over(scale[:, 1, :]), ALU.mult))
                    split_y(ts, l)
                elif l == 2:
                    split_y(hs, l)
                else:
                    split_y(ts, l)
                for g in range(GROUPS):
                    b, n = g % 2, min(4, TILES - 4 * g)
                    G = GROUPS * l + g
                    v.wait_ge(s_agg, G + 1)
                    if G >= 2:
                        v.wait_ge(s_proj, G - 1)
                    dve.tensor_copy(t3[0:65, b, 0:P * n], ps3[b][0:65, 0:P * n]).then_inc(s_t3, 1)
                    v.wait_ge(s_proj, G + 1)
                    o = po[b].rearrange("p (t w) -> p t w", w=P)
                    tt = slice(4 * g, 4 * g + n)
                    sc = scale[:, min(l, 2), tt]
                    if l == 0:
                        link(dve.tensor_copy(cnt[:, tt], o[:, 0:n, 64]))
                        link(dve.tensor_scalar(scale[:, 0, tt], cnt[:, tt], 1.0, None, ALU.max))
                        link(dve.reciprocal(scale[:, 0, tt], scale[:, 0, tt]))
                    dve.tensor_tensor(ts[:, tt, :], o[:, 0:n, 0:FEAT], sc.unsqueeze(2).broadcast_to([P, n, FEAT]),
                                      ALU.mult).then_inc(s_used, 1)
                v.wait_ge(s_used, GROUPS * (l + 1) + 2)
                if l == 0:
                    v.wait_ge(s_e16, 16 * TILES)
                    dve.tensor_tensor(ecat[:, :, 0:EDGE_D], ecat[:, :, 0:EDGE_D],
                                      ecat[:, :, EDGE_D:EDGE_D + 1].broadcast_to([P, TILES, EDGE_D]),
                                      ALU.mult).then_inc(s_cat, 1)
                    d24 = adj[:, 0:(TILES - 1) * (NPAD + P)].rearrange("p (k d) -> p k d", k=TILES - 1)[:, :, 0:P]
                    link(dve.tensor_tensor(d24, d24, ident16[:, :].unsqueeze(1).broadcast_to([P, TILES - 1, P]), ALU.add))
                    dl = A3[:, TILES - 1, NPAD - P:NPAD]
                    link(dve.tensor_tensor(dl, dl, ident16[:, :], ALU.add))
                    link(dve.tensor_scalar(scale[:, 2, :], cnt[:, :], 1.0, None, ALU.add))
                    link(dve.reciprocal(scale[:, 2, :], scale[:, 2, :]))
                    dve.tensor_copy(stat[:, 1, :], scale[:, 2, :]).then_inc(s_var, 1)
                    n_std[0] += 1
                    v.wait_ge(s_std, n_std[0])
                    link(dve.tensor_copy(scale[:, 1, :], stat[:, 2, :]))
                    link(dve.tensor_tensor(xs, xs, ts, ALU.add))
                    for g in range(GROUPS):
                        n = min(4, TILES - 4 * g)
                        v.wait_ge(s_catO, g + 1)
                        dve.tensor_tensor(xs[:, 4 * g:4 * g + n, :], xs[:, 4 * g:4 * g + n, :],
                                          bank(0, FEAT * n).rearrange("p (t f) -> p t f", f=FEAT),
                                          ALU.add).then_inc(s_catU, 1)
                    v.wait_ge(s_catU, GROUPS)
                elif l == 1:
                    link(dve.tensor_tensor(xs, xs, ts, ALU.add))
                    link(dve.tensor_tensor(xs, xs, vecs[:, 0:1, :].broadcast_to(wide), ALU.add))
                elif l == 4:
                    link(dve.tensor_tensor(xs, xs, ts, ALU.add))
            dve.memset(t12[FEAT:FEAT + 1, :, :], 1.0)
            layernorm_relu()
            v.sem_inc(s_cat, 1)
            dve.memset(w_edge, 0.0).then_inc(s_wb0, 1)
            pf = pq[:, :, 0:P]
            p3 = M["p3"].rearrange("p (t k w) -> p t k w", t=TILES, k=3)
            for t in range(TILES):
                v.wait_ge(s_catO, GROUPS + t + 1)
                dve.tensor_copy(pq[:, t, :], bank(t % 4, 2 * P)).then_inc(s_catU, 1)
            v.wait_ge(s_catU, GROUPS + TILES)
            v.sem_inc(s_add, 2)
            dve.memset(M["zeros"], 0.0)
            v.sem_inc(s_pf, 1)
            v.wait_ge(s_io3, 1)
            upto = M["is_upto"][0:1, :].rearrange("p (s t) -> p s t", t=TILES)
            big = [1, SPANS, TILES]
            link(dve.tensor_tensor(upto, M["span_no"][0:1, :].unsqueeze(2).broadcast_to(big),
                                   span0[0:1, :].unsqueeze(1).broadcast_to(big), ALU.is_ge))
            v.wait_ge(s_pa, 1)
            dve.tensor_tensor(pf, pf, p3[:, :, 0, :], ALU.subtract).then_inc(s_pf, 1)
            link(dve.tensor_reduce(M["tile_f"][0:1, :], upto, AX.X, ALU.add))
            link(dve.tensor_scalar(M["tile_f"][0:1, :], M["tile_f"][0:1, :], -1.0, None, ALU.add))
            link(dve.tensor_copy(M["tile_of"][0:1, :], M["tile_f"][0:1, :]))
            dve.tensor_copy(M["lane"], M["lane_i"])
            v.wait_ge(s_pa, 2)
            dve.tensor_tensor(p3[:, :, 2, :], pf, p3[:, :, 1, :], ALU.subtract).then_inc(s_p3, 1)
            v.wait_ge(s_p3, 1)
            def source_rows(i, k):
                v.wait_ge(s_pay[k % 4], (i + k // 4) * 16 + 16)
                v.wait_ge(s_sc, i * 4 + (k + 1))
                big = [P, 4, P]
                dve.tensor_tensor(M["oh"][:, 512 * (k % 4):512 * (k % 4) + 512].rearrange("p (c n) -> p c n", c=4),
                                  M["lane"].unsqueeze(1).broadcast_to(big),
                                  pay_of(k % 4)[:, :, EDGE_F:EDGE_F + 1].broadcast_to(big),
                                  ALU.is_equal).then_inc(s_oh3, 1)

            def add_rows(i, k):
                b = k % 2
                v.wait_ge(s_z, i * 4 + (k + 1))
                v.wait_ge(s_g[b], (i * 2 + k // 2) * 64 + 64)
                dve.tensor_tensor(pair_of("z", b, 512), bank(4 + 3 * b), pair_of("gq", b, 512),
                                  ALU.add).then_inc(s_add, 1)

            def by_chunk(name, b, n):
                return pair_of(name, b, 4 * n).rearrange("p (c w) -> p c w", w=n)

            def softplus(i, k):
                b = k % 2
                z3, ln3 = by_chunk("z", b, P), by_chunk("ln", b, P)
                v.wait_ge(s_ln, i * 4 + (k + 1))
                dve.scalar_tensor_tensor(by_chunk("val", b, FEAT), z3[:, :, FEAT:P], 0.0, ln3[:, :, FEAT:P],
                                         ALU.max, ALU.add)
                dve.scalar_tensor_tensor(by_chunk("gate", b, FEAT), z3[:, :, 0:FEAT], 0.0, ln3[:, :, 0:FEAT],
                                         ALU.min, ALU.subtract).then_inc(s_ga, 1)

            def message(i, k):
                b = k % 2
                hm, m1, m2, m3 = M["hm"], *(pair_of(m, b, 256) for m in ("m1", "m2", "m3"))
                v.wait_ge(s_gt, i * 4 + (k + 1))
                dve.tensor_tensor(hm, pair_of("gate", b, 256), pair_of("val", b, 256), ALU.mult).then_inc(s_hm, 1)
                v.wait_ge(s_sc, i * 4 + (k + 3))
                v.wait_ge(s_hm, i * 4 + (k + 1))
                dve.tensor_copy(m1, hm).then_inc(s_m1, 1)
                v.wait_ge(s_m1, i * 4 + (k + 1))
                dve.tensor_tensor(hm, hm, m1, ALU.subtract).then_inc(s_r1, 1)
                v.wait_ge(s_r1, i * 4 + (k + 1))
                dve.tensor_copy(m2, hm).then_inc(s_m2, 1)
                v.wait_ge(s_m2, i * 4 + (k + 1))
                dve.tensor_tensor(m3, hm, m2, ALU.subtract).then_inc(s_m3, 1)

            source_rows(0, 0)
            source_rows(0, 1)
            add_rows(0, 0)
            with v.Fori(0, SPANS // 4) as i:
                for k in range(4):
                    source_rows(i, k + 2)
                    softplus(i, k)
                    add_rows(i, k + 1)
                    message(i, k)
            softplus(SPANS // 4, 0)
            add_rows(SPANS // 4, 1)
            message(SPANS // 4, 0)
            softplus(SPANS // 4, 1)
            message(SPANS // 4, 1)
            link(dve.tensor_tensor(xs, xs, hs, ALU.add))
            v.wait_ge(s_tile, 1)
            msg = M["msg"].rearrange("p (t f) -> p t f", f=FEAT)
            dve.tensor_copy(M["msg"], ps[:, 0:TILES * FEAT]).then_inc(s_msg, 1)
            v.wait_ge(s_sum, 1)
            link(dve.tensor_scalar(bn[:, 0, :], bank(6, FEAT), -1.0 / N_NODES, None, ALU.mult))
            link(dve.tensor_tensor(msg, msg, bn[:, 0:1, :].broadcast_to(wide), ALU.add))
            dve.tensor_tensor(ts, msg, msg, ALU.mult).then_inc(s_sq, 1)
            v.wait_ge(s_sqs, 1)
            dve.tensor_scalar(bn[:, 1, :], bank(7, FEAT), 1.0 / N_NODES, 1e-5, ALU.mult, ALU.add).then_inc(s_bnv, 1)
            v.wait_ge(s_bns, 1)
            link(dve.reciprocal(bn[:, 2, :], bn[:, 2, :]))
            link(dve.tensor_tensor(bn[:, 2, :], bn[:, 2, :], vecs[:, 1, :], ALU.mult))
            link(dve.tensor_tensor(msg, msg, bn[:, 2:3, :].broadcast_to(wide), ALU.mult))
            link(dve.tensor_tensor(msg, msg, vecs[:, 2:3, :].broadcast_to(wide), ALU.add))
            dve.tensor_tensor(xs, xs, msg, ALU.add).then_inc(s_fin, 1)

        @block.scalar
        def _(act):
            a = nc.scalar
            a.preload_act_table(ACT.Sqrt)
            for t in range(TILES):
                act.wait_ge(s_tiles, t + 1)
                last = a.activation(oh_tile[:, t, :], oh_tile[:, t, :], ACT.Identity,
                                    accum_out=R["counts"][:, t:t + 1])
            last.then_inc(s_counts, 1)
            act.sem_inc(s_seen_a, 2)

            def keep_counts(u, b):
                act.wait_ge(s_seen_c, u + 3)
                n = BLOCK // 2 * TILES
                a.copy(S["seen"][:, ds(u * n, n)], bank(4 + b, n)).then_inc(s_seen_a, 1)

            with act.Fori(0, CHUNKS // (2 * BLOCK)) as i:
                for b in range(2):
                    keep_counts(i * 2 + b, b)
            keep_counts(CHUNKS // BLOCK - 1, 0)
            act.wait_ge(s_ready, 1)
            act.sem_inc(s_adj, 2)

            def low_rows(base, first, before, j):
                for h in range(2):
                    act.wait_ge(s_chunk, (before + j) * 4 + (2 * h + 2))
                    for c in range(2 * h, 2 * h + 2):
                        last = a.activation(lo_far[:, c, :], base, ACT.Abs, scale=-1.0,
                                            bias=B["key_lo"][:, chunk_of(first, j, c)])
                    last.then_inc(s_far, 1)
                    act.wait_ge(s_far, (before + j) * 2 + (h + 1))
                    a.activation(oh_lo[:, 2 * h:2 * h + 2, :], lo_far[:, 2 * h:2 * h + 2, :], ACT.Relu,
                                 scale=-1.0, bias=1.0).then_inc(s_lo, 1)

            def window_copy(b, w):
                act.wait_ge(s_win, w + 1)
                a.copy(A3[:, :, ds(w * WIN, WIN)],
                       adj_acc[b].rearrange("p (k d) -> p k d", d=WIN)).then_inc(s_adj, 1)

            lo_base = [B["lo_base"][:, P * b:P * (b + 1)] for b in range(2)]

            def window_base(b, w):
                a.activation(lo_base[b], B["iota_f"], ACT.Identity, bias=wgrid[:, 2, ds(w, 1)]).then_inc(s_base, 1)

            with act.Fori(0, WINDOWS // RUN) as i:
                trip_now = window_trip(act, i * RUN)
                window_base(0, i * RUN)
                for s in range(RUN):
                    b, w, trip_next = s % 2, i * RUN + s, []
                    first, count, before = trip_now
                    act.wait_ge(s_base, w + 1)
                    low_rows(lo_base[b], first, before, 0)
                    if s:
                        window_copy(1 - b, w - 1)
                    if s + 1 < RUN:
                        window_base(1 - b, w + 1)
                        trip_next.append(trip_value(act, w + 1, 0))
                    low_rows(lo_base[b], first, before, 1)
                    if s + 1 < RUN:
                        trip_next.append(trip_value(act, w + 1, 1))
                    with act.Fori(2, count) as j:
                        low_rows(lo_base[b], first, before, j)
                    if s + 1 < RUN:
                        trip_now = trip_next + [trip_value(act, w + 1, 2)]
                window_copy(1, i * RUN + RUN - 1)
            n_var = [0]

            def root():
                n_var[0] += 1
                act.wait_ge(s_var, n_var[0])
                a.activation(stat[:, 2, :], stat[:, 1, :], ACT.Sqrt).then_inc(s_std, 1)

            def cat_group(at, with_last):
                g = at % GROUPS
                b, n = g % 2, min(4, TILES - 4 * g)
                act.wait_ge(s_catT, at + 1)
                if with_last:
                    a.copy(t3[0:ECAT, b, 0:P * n], bank(7)[0:ECAT, 0:P * n])
                a.copy(t12[0:FEAT, b, 0:P * n], bank(6)[0:FEAT, 0:P * n]).then_inc(s_catS, 1)

            for l in range(LAYERS):
                if l < 3:
                    root()
                for g in range(GROUPS):
                    b, n = g % 2, min(4, TILES - 4 * g)
                    G = GROUPS * l + g
                    act.wait_ge(s_agg, G + 1)
                    if G >= 2:
                        act.wait_ge(s_proj, G - 1)
                    a.copy(t12[:, b, 0:P * n], bank(b, P * n)).then_inc(s_t12, 1)
                if l == 0:
                    root()
                    for g in range(GROUPS):
                        cat_group(g, True)
            root()
            for g in range(GROUPS):
                cat_group(GROUPS + g, False)
            p3 = M["p3"].rearrange("p (t k w) -> p t k w", t=TILES, k=3)
            for part in range(2):
                act.wait_ge(s_pf, part + 1)
                a.copy(p3[:, :, part, :], pq[:, :, 0:P]).then_inc(s_pa, 1)
            a.preload_act_table_set("natural_log_exp_and_others")
            def turned(i, k):
                b = k % 2
                act.wait_ge(s_tr, i * 4 + (k + 5))
                if k >= 2:
                    act.wait_ge(s_z, i * 4 + (k - 1))
                a.copy(pair_of("oht", b, 512), bank(5))
                a.copy(pair_of("et", b, 2 * P)[0:2 * PAYLOAD, :], bank(6, 2 * P)[0:2 * PAYLOAD, :]).then_inc(s_ct, 1)

            def logs(i, k):
                b = k % 2
                z, ab = pair_of("z", b, 512), pair_of("ab", b, 512)
                act.wait_ge(s_add, i * 4 + (k + 3))
                a.activation(ab, z, ACT.Abs).then_inc(s_ab, 1)
                act.wait_ge(s_ab, i * 4 + (k + 1))
                a.activation(ab, ab, ACT.Exp, scale=-1.0).then_inc(s_ex, 1)
                act.wait_ge(s_ex, i * 4 + (k + 1))
                a.activation(pair_of("ln", b, 512), ab, ACT.Ln, bias=1.0).then_inc(s_ln, 1)

            def gate(i, k):
                g = pair_of("gate", k % 2, 256)
                act.wait_ge(s_ga, i * 4 + (k + 1))
                a.activation(g, g, ACT.Exp).then_inc(s_gt, 1)

            turned(0, 0)
            turned(0, 1)
            logs(0, 0)
            with act.Fori(0, SPANS // 4) as i:
                for k in range(4):
                    gate(i, k)
                    turned(i, k + 2)
                    logs(i, k + 1)
            gate(SPANS // 4, 0)
            logs(SPANS // 4, 1)
            gate(SPANS // 4, 1)
            act.wait_ge(s_bnv, 1)
            a.activation(bn[:, 2, :], bn[:, 1, :], ACT.Sqrt).then_inc(s_bns, 1)

        @block.tensor
        def _(pe):
            mm = nc.tensor.matmul
            pe.wait_ge(s_hit, 1)
            r = slice(0, BOUND_ROWS)
            for a in range(2):
                for q in range(CPR):
                    at = 1024 * a + 512 * (q // (CPR // 2)) + q % (CPR // 2) * BOUND_ROWS
                    last = mm(ps[0:WINDOWS, at:at + BOUND_ROWS],
                              hit[r, q, a, :], ident[r, 0:BOUND_ROWS], start=True, stop=True)
            last.then_inc(s_hitT, 1)
            pe.wait_ge(s_ext, 1)
            for a in range(2):
                last = mm(ps[0:1, 2048 + WINDOWS * a:2048 + WINDOWS * (a + 1)], ext[:, a:a + 1],
                          ident[0:WINDOWS, 0:WINDOWS], start=True, stop=True)
            last.then_inc(s_extT, 1)
            pe.wait_ge(s_counts, 1)
            mm(bank(3)[:, 0:TILES], ones[:, :], R["counts"], start=True, stop=True)
            mm(bank(3)[:, 64:64 + TILES], E["before"], R["counts"], start=True, stop=True).then_inc(s_pre, 1)
            dlo2, dhi2 = (S[k].rearrange("p (b c n) -> p b c n", b=2, c=BLOCK) for k in ("oh_dlo", "oh_dhi"))

            def count_block(u, b):
                pe.wait_ge(s_seen_a, u + 1)
                pe.wait_ge(s_seen_o, u + 1)
                for r in range(BLOCK // 2):
                    for h in range(2):
                        o = bank(4 + b)[WIN * h:WIN * (h + 1), TILES * r:TILES * (r + 1)]
                        for c in range(2):
                            last = mm(o, dlo2[:, b, 2 * r + c, :], dhi2[:, b, 2 * r + c, TILES * h:TILES * (h + 1)],
                                      start=(c == 0), stop=(c == 1))
                last.then_inc(s_seen_c, 1)

            with pe.Fori(0, CHUNKS // (2 * BLOCK)) as i:
                for b in range(2):
                    count_block(i * 2 + b, b)
            count_block(CHUNKS // BLOCK - 1, 0)
            pe.wait_ge(s_ready, 1)
            pe.sem_inc(s_chunk, 4)

            def window_chunks(b, first, before, j, start):
                for a in range(4):
                    if a % 2 == 0:
                        pe.wait_ge(s_lo, (before + j) * 2 + (a // 2 + 1))
                    pe.wait_ge(s_oh, (before + j) * 4 + (a + 1))
                    for lo in range(0, MOV, 512):
                        n = min(512, MOV - lo)
                        last = mm(adj_acc[b][:, lo:lo + n], oh_lo[:, a, :], oh_mv[:, a, lo:lo + n],
                                  start=start and a == 0, stop=False)
                    last.then_inc(s_chunk, 1)

            with pe.Fori(0, WINDOWS // RUN) as i:
                trip_now = window_trip(pe, i * RUN)
                for s in range(RUN):
                    b, w, trip_next = s % 2, i * RUN + s, []
                    first, count, before = trip_now
                    pe.wait_ge(s_adj, w + 1)
                    for j in range(2):
                        window_chunks(b, first, before, j, j == 0)
                        if s + 1 < RUN:
                            trip_next.append(trip_value(pe, w + 1, j))
                    with pe.Fori(2, count) as j:
                        window_chunks(b, first, before, j, False)
                    for lo in range(0, MOV, 512):
                        last = mm(adj_acc[b][:, lo:lo + 1], zeros[:, :], zeros[:, 0:1], start=False, stop=True)
                    last.then_inc(s_win, 1)
                    if s + 1 < RUN:
                        trip_now = trip_next + [trip_value(pe, w + 1, 2)]

            def aggregate(l, g):
                b, n = g % 2, min(4, TILES - 4 * g) * P
                G = GROUPS * l + g
                if G >= 2:
                    pe.wait_ge(s_t12, G - 1)
                    pe.wait_ge(s_t3, G - 1)
                for k in range(TILES):
                    mm(bank(b, n), y12[:, k, :], A3[:, k, 512 * g:512 * g + n], start=(k == 0), stop=(k == TILES - 1))
                if g == 0:
                    pe.wait_ge(s_y3, l + 1)
                for k in range(TILES):
                    last = mm(bank(2 + b)[0:65, 0:n], y3[:, k, 0:65], A3[:, k, 512 * g:512 * g + n],
                              start=(k == 0), stop=(k == TILES - 1))
                last.then_inc(s_agg, 1)

            def project(l, g):
                b = g % 2
                G = GROUPS * l + g
                pe.wait_ge(s_t12, G + 1)
                pe.wait_ge(s_t3, G + 1)
                pe.wait_ge(s_used, G + 1)
                for i in range(min(4, TILES - 4 * g)):
                    o = ps[:, 512 * (4 + b) + P * i:512 * (4 + b) + P * i + 65]
                    mm(o, t12[:, b, P * i:P * (i + 1)], w12[:, l, :], start=True, stop=False)
                    last = mm(o, t3[0:65, b, P * i:P * (i + 1)], w3[:, l, :], start=False, stop=True)
                last.then_inc(s_proj, 1)

            def cat_group(at, with_last):
                g = at % GROUPS
                n = min(4, TILES - 4 * g)
                for i in range(n):
                    last = nc.tensor.transpose(bank(6)[0:FEAT, P * i:P * (i + 1)], hs[:, 4 * g + i, :], ident[:, :])
                    if with_last:
                        last = nc.tensor.transpose(bank(7)[0:ECAT, P * i:P * (i + 1)], ecat[:, 4 * g + i, :], ident[:, :])
                last.then_inc(s_catT, 1)
                pe.wait_ge(s_catS, at + 1)

            pe.wait_ge(s_w, 16 * n_weights)
            pe.sem_inc(s_used, 2)
            for l in range(LAYERS):
                pe.wait_ge(s_y, l + 1)
                if l == 1:
                    pe.wait_ge(s_catU, GROUPS)
                for g in range(GROUPS):
                    aggregate(l, g)
                    if g:
                        project(l, g - 1)
                project(l, GROUPS - 1)
                if l == 0:
                    pe.wait_ge(s_cat, 1)
                    for g in range(GROUPS):
                        b, n = g % 2, min(4, TILES - 4 * g)
                        cat_group(g, True)
                        if g:
                            pe.wait_ge(s_catU, g)
                        for i in range(n):
                            o = bank(0)[:, FEAT * i:FEAT * (i + 1)]
                            mm(o, t12[0:FEAT, b, P * i:P * (i + 1)], wroot[:, :], start=True, stop=False)
                            last = mm(o, t3[0:ECAT, b, P * i:P * (i + 1)], wlast[:, :], start=False, stop=True)
                        last.then_inc(s_catO, 1)
            pe.wait_ge(s_cat, 2)
            def turn_nodes(g):
                for i in range(min(4, TILES - 4 * g)):
                    last = nc.tensor.transpose(bank(6)[0:FEAT, P * i:P * (i + 1)], hs[:, 4 * g + i, :], ident[:, :])
                last.then_inc(s_catT, 1)

            turn_nodes(0)
            for g in range(GROUPS):
                b, n = g % 2, min(4, TILES - 4 * g)
                pe.wait_ge(s_catS, GROUPS + g + 1)
                if g + 1 < GROUPS:
                    turn_nodes(g + 1)
                for i in range(n):
                    t = 4 * g + i
                    if t >= 4:
                        pe.wait_ge(s_catU, GROUPS + t - 3)
                    mm(bank(t % 4, 4 * FEAT), t12[0:FEAT + 1, b, P * i:P * (i + 1)], wpq[:, :],
                       start=True, stop=True).then_inc(s_catO, 1)
            pe.sem_inc(s_tr, 4)
            pe.wait_ge(s_p3, 1)
            pe.wait_ge(s_wb, 16 * 4)
            for k in range(4):
                mm(bank(k), M["zeros"][:, 0:P], M["zeros"][:, 0:512], start=True, stop=False)
            pe.sem_inc(s_sc, 4)

            def turn(i, k):
                slot = k % 4
                pe.wait_ge(s_oh3, i * 4 + (k + 1))
                if k >= 1:
                    pe.wait_ge(s_ct, i * 4 + k)
                for c in range(4):
                    mm(bank(5)[:, P * c:P * (c + 1)], M["oh"][:, 512 * slot + P * c:512 * slot + P * (c + 1)],
                       ident16[:, :], start=True, stop=True)
                for h in range(2):
                    last = nc.tensor.transpose(bank(6)[0:2 * PAYLOAD, P * h:P * (h + 1)],
                                               pay(slot)[:, 2 * PAYLOAD * h:2 * PAYLOAD * (h + 1)], ident[:, :])
                last.then_inc(s_tr, 1)

            def products(i, k):
                b = k % 2
                tile = group_tile(pe, i, k)
                pe.wait_ge(s_ct, i * 4 + (k + 1))
                pe.wait_ge(s_add, i * 4 + (k + 1))
                for c in range(4):
                    o = bank(4 + 3 * b)[:, P * c:P * (c + 1)]
                    if c % 2 == 0:
                        mm(bank(4 + 3 * b)[:, P * c:P * (c + 2)], pair_of("et", b, 2 * P)[0:2 * PAYLOAD, P * (c // 2):P * (c // 2 + 1)],
                           w_edge, start=True, stop=False)
                    for part in range(3):
                        last = mm(o, pair_of("oht", b, 512)[:, P * c:P * (c + 1)],
                                  M["p3"][:, ds(tile * (3 * P) + P * part, P)], start=False,
                                  stop=(c % 2 == 1 and part == 2))
                last.then_inc(s_z, 1)

            def scatter(i, k):
                b, slot = k % 2, k % 4
                tile = group_tile(pe, i, k)
                pe.wait_ge(s_m3, i * 4 + (k + 1))
                for c in range(4):
                    for part in ("m1", "m2", "m3"):
                        last = mm(ps[:, ds(tile * FEAT, FEAT)], M["oh"][:, 512 * slot + P * c:512 * slot + P * (c + 1)],
                                  pair_of(part, b, 256)[:, FEAT * c:FEAT * (c + 1)], start=False, stop=False)
                last.then_inc(s_sc, 1)

            turn(0, 0)
            products(0, 0)
            turn(0, 1)
            products(0, 1)
            turn(0, 2)
            whole = (SPANS - 3) // 4
            with pe.Fori(0, whole) as i:
                for k in range(4):
                    products(i, k + 2)
                    turn(i, k + 3)
                    scatter(i, k)
            for k in range(SPANS - 4 * whole):
                if 4 * whole + k + 2 < SPANS:
                    products(whole, k + 2)
                if 4 * whole + k + 3 < SPANS:
                    turn(whole, k + 3)
                scatter(whole, k)
            for k in range(4):
                last = mm(ps[:, 512 * k:512 * k + 1], M["zeros"][:, 0:P], M["zeros"][:, 0:1], start=False, stop=True)
            last.then_inc(s_tile, 1)
            msg = M["msg"].rearrange("p (t f) -> p t f", f=FEAT)
            pe.wait_ge(s_msg, 1)
            for t in range(TILES):
                last = mm(bank(6, FEAT), ones[:, :], msg[:, t, :], start=(t == 0), stop=(t == TILES - 1))
            last.then_inc(s_sum, 1)
            pe.wait_ge(s_sq, 1)
            for t in range(TILES):
                rows = P if t < TILES - 1 else LAST
                last = mm(bank(7, FEAT), ones[0:rows, :], ts[0:rows, t, :], start=(t == 0), stop=(t == TILES - 1))
            last.then_inc(s_sqs, 1)


def kernel(x, src, dst, edge_attr_16, edge_attr_32, L0_gnn_W_l, L0_gnn_b_l, L0_gnn_W_r, L0_gnn_W_e, L0_gnn_b_e,
           L1_gnn_W, L1_gnn_b, L2_gnn_weights, L3_gnn_W_f, L3_gnn_b_f, L3_gnn_W_s, L3_gnn_b_s, L3_gnn_gamma,
           L3_gnn_beta):
    import numpy as np
    import concourse.bacc as bacc
    from concourse.bass_utils import run_bass_kernel_spmd

    def padded(a, size, value):
        a = np.asarray(a)
        wide = np.full((size,) + a.shape[1:], value, a.dtype)
        wide[:a.shape[0]] = a
        return wide

    src_rows = padded(src, CHUNKS * P, PAD).reshape(CHUNKS, P)
    dst_rows = padded(dst, CHUNKS * P, PAD).reshape(CHUNKS, P)
    row = lambda a: np.asarray(a).reshape(1, FEAT)
    w2 = np.asarray(L2_gnn_weights)
    arrays = {
        "x": padded(x, NPAD, 0),
        "src_cols": src_rows.T, "dst_cols": dst_rows.T, "dst_rows": dst_rows,
        "e16": edge_attr_16, "e32": padded(edge_attr_32, CHUNKS * P, 0),
        "sage_wl": L0_gnn_W_l, "sage_bl": row(L0_gnn_b_l), "sage_wr": L0_gnn_W_r, "sage_we": L0_gnn_W_e,
        "sage_be": row(L0_gnn_b_e), "gcn_w": L1_gnn_W, "gcn_b": row(L1_gnn_b),
        "mean_wt": w2.transpose(0, 2, 1).reshape(3 * FEAT, FEAT),
        "wf": L3_gnn_W_f, "bf": row(L3_gnn_b_f), "ws": L3_gnn_W_s, "bs": row(L3_gnn_b_s),
        "gamma": row(L3_gnn_gamma), "beta": row(L3_gnn_beta),
    }
    arrays = {f"in_{k}": np.ascontiguousarray(a) for k, a in arrays.items()}
    nc = bacc.Bacc("TRN2", target_bir_lowering=False, num_devices=1)
    args = [nc.dram_tensor(k, a.shape, mybir.dt.from_np(a.dtype), kind="ExternalInput").ap()
            for k, a in arrays.items()]
    args.append(nc.dram_tensor("out_x", (N_NODES, FEAT), mybir.dt.float32, kind="ExternalOutput").ap())
    gnn_program(nc, *args)
    result = run_bass_kernel_spmd(nc, [arrays], core_ids=[0])
    return result.results[0]["out_x"]
```
